# Optimizing a Trainium2 kernel written in Bass

```python
import numpy as np
import jax
import jax.numpy as jnp

def _softmax(x, axis=-1):
    return jax.nn.softmax(x, axis=axis)

def _gelu(x):
    return jax.nn.gelu(x, approximate=True)

def _silu(x):
    return jax.nn.silu(x)

def _sigmoid(x):
    return jax.nn.sigmoid(x)

def _layernorm(x, axis=-1, eps=1e-05):
    m = jnp.mean(x, axis=axis, keepdims=True)
    v = jnp.var(x, axis=axis, keepdims=True)
    return (x - m) / jnp.sqrt(v + eps)

def _scatter_add(tgt, idx, src, axis=0):
    return tgt.at[idx].add(src)

def _segment_sum(src, seg, n):
    return jax.ops.segment_sum(src, seg, n)
kernel_name = 'mk_xattn_ffn_d4_seqx_r8_cc9716'

def setup_inputs(seed: int=0):
    np.random.seed(seed)
    _w = jnp.asarray

    def _rec_inputs():
        import jax
        import jax.numpy as jnp
        _rk = jax.random.key(seed)
        x = -0.0003929 + 0.9999 * jax.random.normal(jax.random.fold_in(_rk, 1), (16, 128, 256), jnp.float32)
        _lenS = 128 - jax.random.randint(jax.random.fold_in(_rk, 7), (16,), 0, max(1, 128 // 4) + 1, jnp.int32)
        _lenS2 = 128 - jax.random.randint(jax.random.fold_in(_rk, 8), (16,), 0, max(1, 128 // 4) + 1, jnp.int32)
        _ctx_2048P = jax.random.normal(jax.random.fold_in(_rk, 11), (16, 16, 256), jnp.float32)
        _ctx_2048c = jax.random.dirichlet(jax.random.fold_in(_rk, 511), 0.3 * jnp.ones((16,), jnp.float32), (16, 128))
        _ctx_2048t = jnp.einsum('bsk,bkd->bsd', _ctx_2048c, _ctx_2048P)
        _ctx_2048t = _ctx_2048t * jax.lax.rsqrt(jnp.mean(jnp.square(_ctx_2048t)) + 1e-12) * 0.953939
        ctx_2048 = -0.000514642 + 1.00011 * (_ctx_2048t + 0.3 * jax.random.normal(jax.random.fold_in(_rk, 611), (16, 128, 256), jnp.float32))
        _validS = jnp.arange(128)[None, :] < _lenS[:, None]
        _validS2 = jnp.arange(128)[None, :] < _lenS2[:, None]
        _causal = jnp.tril(jnp.ones((128, 128), dtype=bool))
        mask_BxS2_bk0 = jnp.logical_not(jnp.broadcast_to(_validS2[:, :], (16, 128)))
        return (x, ctx_2048, mask_BxS2_bk0)
    x, ctx_2048, mask_BxS2_bk0 = _rec_inputs()

    def _L0_xattn_setup():
        import jax, jax.numpy as jnp
        import numpy as np
        NUM_HEADS = 16

        def _qdq(x):
            s = jnp.maximum(jnp.max(jnp.abs(x), axis=-1, keepdims=True) / 127.0, 1e-08)
            return jnp.clip(jnp.round(x / s), -127.0, 127.0) * s
        key = jax.random.key(seed)
        ks = jax.random.split(key, 8)
        B, N, M, D = (2, 512, 64, 256)
        w_std = 0.02
        return {'x': jax.random.normal(ks[0], (B, N, D), jnp.float32), 'cond': jax.random.normal(ks[1], (B, M, D), jnp.float32), 'wq': jax.random.normal(ks[2], (D, D), jnp.float32) * w_std, 'bq': jax.random.normal(ks[3], (D,), jnp.float32) * w_std, 'wkv': jax.random.normal(ks[4], (2 * D, D), jnp.float32) * w_std, 'bkv': jax.random.normal(ks[5], (2 * D,), jnp.float32) * w_std, 'wp': jax.random.normal(ks[6], (D, D), jnp.float32) * w_std, 'bp': jax.random.normal(ks[7], (D,), jnp.float32) * w_std}
    _L0_xattn_all = _L0_xattn_setup()
    _L0_xattn_in = {k: v for k, v in _L0_xattn_all.items() if k in ('wq', 'bq', 'wkv', 'bkv', 'wp', 'bp')}
    del _L0_xattn_all

    def _L0_ffn_setup():
        import jax, jax.numpy as jnp
        import numpy as np
        ROPE_THETA = 1000000.0
        TOP_K = 2

        def rmsnorm(x, w, eps=1e-06):
            xf = x.astype(jnp.float32)
            n = jax.lax.rsqrt(jnp.mean(xf * xf, axis=-1, keepdims=True) + eps)
            return (xf * n).astype(x.dtype) * w

        def rope_tables(seq_len, head_dim):
            freqs = 1.0 / ROPE_THETA ** (jnp.arange(0, head_dim, 2, dtype=jnp.float32) / head_dim)
            t = jnp.arange(seq_len, dtype=jnp.float32)
            f = jnp.outer(t, freqs)
            return (jnp.cos(f), jnp.sin(f))

        def apply_rope(x, cos, sin):
            half = x.shape[-1] // 2
            x1, x2 = (x[..., :half], x[..., half:])
            c = cos[None, None]
            s = sin[None, None]
            return jnp.concatenate([x1 * c - x2 * s, x2 * c + x1 * s], axis=-1)
        key = jax.random.key(seed)
        ks = jax.random.split(key, 8)
        B, S, D = (2, 256, 256)
        Hq, Hkv, hd = (16, 4, 128)
        E, I = (8, 176)
        sc = 0.02
        return {'hidden': jax.random.normal(ks[0], (B, S, D), jnp.float32), 'attn_norm_w': jnp.ones((D,), jnp.float32), 'q_w': jax.random.normal(ks[1], (Hq * hd, D), jnp.float32) * sc, 'k_w': jax.random.normal(ks[2], (Hkv * hd, D), jnp.float32) * sc, 'v_w': jax.random.normal(ks[3], (Hkv * hd, D), jnp.float32) * sc, 'o_w': jax.random.normal(ks[4], (D, Hq * hd), jnp.float32) * sc, 'q_norm_w': jnp.ones((hd,), jnp.float32), 'k_norm_w': jnp.ones((hd,), jnp.float32), 'ffn_norm_w': jnp.ones((D,), jnp.float32), 'gate_w': jax.random.normal(ks[5], (E, D), jnp.float32) * sc, 'wg': jax.random.normal(ks[6], (E, I, D), jnp.float32) * sc, 'wu': jax.random.normal(ks[7], (E, I, D), jnp.float32) * sc, 'wd': jax.random.normal(jax.random.fold_in(key, 99), (E, D, I), jnp.float32) * sc}
    _L0_ffn_all = _L0_ffn_setup()
    _L0_ffn_in = {k: v for k, v in _L0_ffn_all.items() if k in ('attn_norm_w', 'q_w', 'k_w', 'v_w', 'o_w', 'q_norm_w', 'k_norm_w', 'ffn_norm_w', 'gate_w', 'wg', 'wu', 'wd')}
    del _L0_ffn_all

    def _L1_xattn_setup():
        import jax, jax.numpy as jnp
        import numpy as np
        key = jax.random.key(seed)
        k1, k2, k3 = jax.random.split(key, 3)
        B, S, D, M = (8, 256, 256, 128)
        hidden_states = jax.random.normal(k1, (B, S, D), dtype=jnp.float32)
        memory_tokens = jax.random.normal(k2, (B, M, D), dtype=jnp.float32)
        memory_mask = jax.random.randint(k3, (B, M), 0, 2).astype(jnp.bool_)
        return {'hidden_states': hidden_states, 'memory_tokens': memory_tokens, 'memory_mask': memory_mask}
    _L1_xattn_all = _L1_xattn_setup()
    _L1_xattn_in = {k: v for k, v in _L1_xattn_all.items() if k in ()}
    del _L1_xattn_all

    def _L1_ffn_setup():
        import jax, jax.numpy as jnp
        import numpy as np
        EPS = 1e-05
        LN_EPS = 1e-06

        def activation_quant(x):
            scale = 127.0 / jnp.clip(jnp.max(jnp.abs(x), axis=-1, keepdims=True), EPS, None)
            return jnp.clip(jnp.round(x * scale), -128.0, 127.0) / scale

        def weight_quant(w):
            scale = 1.0 / jnp.clip(jnp.mean(jnp.abs(w)), EPS, None)
            return jnp.clip(jnp.round(w * scale), -1.0, 1.0) / scale

        def bit_linear(x, w):
            xq = x + jax.lax.stop_gradient(activation_quant(x) - x)
            wq = w + jax.lax.stop_gradient(weight_quant(w) - w)
            return jnp.einsum('bsh,oh->bso', xq, wq)

        def subln(x, g):
            var = jnp.mean(jnp.square(x), axis=-1, keepdims=True)
            return x * jax.lax.rsqrt(var + LN_EPS) * g
        key = jax.random.key(seed)
        k1, k2, k3, k4 = jax.random.split(key, 4)
        H, I = (256, 1024)
        B, S = (4, 256)
        return {'x': jax.random.normal(k1, (B, S, H), dtype=jnp.float32), 'w_gate': jax.random.normal(k2, (I, H), dtype=jnp.float32) * 0.02, 'w_up': jax.random.normal(k3, (I, H), dtype=jnp.float32) * 0.02, 'w_down': jax.random.normal(k4, (H, I), dtype=jnp.float32) * 0.02, 'subln_weight': jnp.ones((I,), dtype=jnp.float32)}
    _L1_ffn_all = _L1_ffn_setup()
    _L1_ffn_in = {k: v for k, v in _L1_ffn_all.items() if k in ('w_gate', 'w_up', 'w_down', 'subln_weight')}
    del _L1_ffn_all

    def _L2_xattn_setup():
        import jax, jax.numpy as jnp
        import numpy as np
        DIM = 256
        NH = 16
        HD = DIM // NH
        EPS = 1e-06
        IMG_LEN = 257

        def rms_norm(x, w, eps=EPS):
            xf = x.astype(jnp.float32)
            y = xf * jax.lax.rsqrt(jnp.mean(xf * xf, axis=-1, keepdims=True) + eps)
            return y.astype(x.dtype) * w

        def linear(x, w, b):
            return jnp.einsum('blc,oc->blo', x, w) + b

        def attention(q, k, v):
            scale = 1.0 / jnp.sqrt(jnp.asarray(HD, q.dtype))
            scores = jnp.einsum('bqhd,bkhd->bhqk', q, k) * scale
            probs = jax.nn.softmax(scores, axis=-1)
            return jnp.einsum('bhqk,bkhd->bqhd', probs, v)
        key = jax.random.key(seed)
        ks = jax.random.split(key, 12)
        B, L = (2, 1024)
        s = 0.02
        inp = {'x': jax.random.normal(ks[0], (B, L, DIM), jnp.float32), 'context': jax.random.normal(ks[1], (B, 769, DIM), jnp.float32), 'q_w': jax.random.normal(ks[2], (DIM, DIM), jnp.float32) * s, 'q_b': jnp.zeros((DIM,), jnp.float32), 'k_w': jax.random.normal(ks[3], (DIM, DIM), jnp.float32) * s, 'k_b': jnp.zeros((DIM,), jnp.float32), 'v_w': jax.random.normal(ks[4], (DIM, DIM), jnp.float32) * s, 'v_b': jnp.zeros((DIM,), jnp.float32), 'k_img_w': jax.random.normal(ks[5], (DIM, DIM), jnp.float32) * s, 'k_img_b': jnp.zeros((DIM,), jnp.float32), 'v_img_w': jax.random.normal(ks[6], (DIM, DIM), jnp.float32) * s, 'v_img_b': jnp.zeros((DIM,), jnp.float32), 'o_w': jax.random.normal(ks[7], (DIM, DIM), jnp.float32) * s, 'o_b': jnp.zeros((DIM,), jnp.float32), 'norm_q_w': jnp.ones((DIM,), jnp.float32), 'norm_k_w': jnp.ones((DIM,), jnp.float32), 'norm_k_img_w': jnp.ones((DIM,), jnp.float32)}
        return inp
    _L2_xattn_all = _L2_xattn_setup()
    _L2_xattn_in = {k: v for k, v in _L2_xattn_all.items() if k in ('q_w', 'q_b', 'k_w', 'k_b', 'v_w', 'v_b', 'k_img_w', 'k_img_b', 'v_img_w', 'v_img_b', 'o_w', 'o_b', 'norm_q_w', 'norm_k_w', 'norm_k_img_w')}
    del _L2_xattn_all

    def _L2_ffn_setup():
        import jax, jax.numpy as jnp
        import numpy as np
        TOPK = 4
        key = jax.random.key(seed)
        k_x, k_a, k_b, k_w, k_bias = jax.random.split(key, 5)
        b, s, h, j, a, r = (4, 256, 256, 256, 64, 16)
        x = jax.random.normal(k_x, (b, s, h), dtype=jnp.float32)
        A = jax.random.normal(k_a, (a, r, h), dtype=jnp.float32) * 0.02
        B = jax.random.normal(k_b, (a, j, r), dtype=jnp.float32) * 0.02
        W = jax.random.normal(k_w, (j, h), dtype=jnp.float32) * 0.02
        bias = jax.random.normal(k_bias, (j,), dtype=jnp.float32) * 0.02
        return {'x': x, 'A': A, 'B': B, 'W': W, 'bias': bias}
    _L2_ffn_all = _L2_ffn_setup()
    _L2_ffn_in = {k: v for k, v in _L2_ffn_all.items() if k in ('A', 'B', 'W', 'bias')}
    del _L2_ffn_all

    def _L3_xattn_setup():
        import jax, jax.numpy as jnp
        import numpy as np
        D_MODEL = 256
        NUM_HEADS = 16
        HEAD_DIM = D_MODEL // NUM_HEADS

        def _fq_sym(x, axis):
            s = jnp.max(jnp.abs(x), axis=axis, keepdims=True) / 127.0
            s = jnp.maximum(s, 1e-08)
            q = jnp.clip(jnp.round(x / s), -127.0, 127.0) * s
            return x + jax.lax.stop_gradient(q - x)

        def _fq_unsigned(x, axis):
            s = jnp.max(x, axis=axis, keepdims=True) / 255.0
            s = jnp.maximum(s, 1e-08)
            q = jnp.clip(jnp.round(x / s), 0.0, 255.0) * s
            return x + jax.lax.stop_gradient(q - x)
        key = jax.random.key(seed)
        ks = jax.random.split(key, 8)
        B, N, M, C = (2, 256, 64, D_MODEL)
        return {'x': jax.random.normal(ks[0], (B, N, C), jnp.float32), 'cond': jax.random.normal(ks[1], (B, M, C), jnp.float32), 'Wq': jax.random.normal(ks[2], (C, C), jnp.float32) * 0.02, 'bq': jnp.zeros((C,), jnp.float32), 'Wkv': jax.random.normal(ks[3], (C, 2 * C), jnp.float32) * 0.02, 'bkv': jnp.zeros((2 * C,), jnp.float32), 'Wp': jax.random.normal(ks[4], (C, C), jnp.float32) * 0.02, 'bp': jnp.zeros((C,), jnp.float32)}
    _L3_xattn_all = _L3_xattn_setup()
    _L3_xattn_in = {k: v for k, v in _L3_xattn_all.items() if k in ('Wq', 'bq', 'Wkv', 'bkv', 'Wp', 'bp')}
    del _L3_xattn_all

    def _L3_ffn_setup():
        import jax, jax.numpy as jnp
        import numpy as np
        H = 256
        I = 176
        E = 8
        TOP_K = 2
        N_SHARED = 2
        I_SH = I * N_SHARED
        NORM_TOPK = True

        def _moe_forward(hidden_states, gate_w, expert_gate, expert_up, expert_down, shared_gate, shared_up, shared_down):
            bsz, seq_len, hdim = hidden_states.shape
            x = hidden_states.reshape(-1, hdim)
            logits = x @ gate_w.T
            probs = jax.nn.softmax(logits, axis=-1)
            routing_weights, selected = jax.lax.top_k(probs, TOP_K)
            if NORM_TOPK:
                routing_weights = routing_weights / (routing_weights.sum(axis=-1, keepdims=True) + 1e-20)
            combine = jnp.sum(jax.nn.one_hot(selected, E, dtype=routing_weights.dtype) * routing_weights[..., None], axis=1)
            g_sh = x @ shared_gate.T
            u_sh = x @ shared_up.T
            out = jax.nn.silu(g_sh) * u_sh @ shared_down.T
            g = jnp.einsum('nh,eih->nei', x, expert_gate)
            u = jnp.einsum('nh,eih->nei', x, expert_up)
            y = jnp.einsum('nei,ehi->neh', jax.nn.silu(g) * u, expert_down)
            out = out + jnp.einsum('neh,ne->nh', y, combine)
            return out.reshape(bsz, seq_len, hdim)
        key = jax.random.key(seed)
        ks = jax.random.split(key, 8)
        s = 0.02
        return {'hidden_states': jax.random.normal(ks[0], (1, 128, H), dtype=jnp.float32), 'gate_w': jax.random.normal(ks[1], (E, H), dtype=jnp.float32) * s, 'expert_gate': jax.random.normal(ks[2], (E, I, H), dtype=jnp.float32) * s, 'expert_up': jax.random.normal(ks[3], (E, I, H), dtype=jnp.float32) * s, 'expert_down': jax.random.normal(ks[4], (E, H, I), dtype=jnp.float32) * s, 'shared_gate': jax.random.normal(ks[5], (I_SH, H), dtype=jnp.float32) * s, 'shared_up': jax.random.normal(ks[6], (I_SH, H), dtype=jnp.float32) * s, 'shared_down': jax.random.normal(ks[7], (H, I_SH), dtype=jnp.float32) * s}
    _L3_ffn_all = _L3_ffn_setup()
    _L3_ffn_in = {k: v for k, v in _L3_ffn_all.items() if k in ('gate_w', 'expert_gate', 'expert_up', 'expert_down', 'shared_gate', 'shared_up', 'shared_down')}
    del _L3_ffn_all
    return {'x': x, 'ctx_2048': ctx_2048, 'mask_BxS2_bk0': mask_BxS2_bk0, 'L0_xattn_wq': _L0_xattn_in['wq'], 'L0_xattn_bq': _L0_xattn_in['bq'], 'L0_xattn_wkv': _L0_xattn_in['wkv'], 'L0_xattn_bkv': _L0_xattn_in['bkv'], 'L0_xattn_wp': _L0_xattn_in['wp'], 'L0_xattn_bp': _L0_xattn_in['bp'], 'L0_ffn_attn_norm_w': _L0_ffn_in['attn_norm_w'], 'L0_ffn_q_w': _L0_ffn_in['q_w'], 'L0_ffn_k_w': _L0_ffn_in['k_w'], 'L0_ffn_v_w': _L0_ffn_in['v_w'], 'L0_ffn_o_w': _L0_ffn_in['o_w'], 'L0_ffn_q_norm_w': _L0_ffn_in['q_norm_w'], 'L0_ffn_k_norm_w': _L0_ffn_in['k_norm_w'], 'L0_ffn_ffn_norm_w': _L0_ffn_in['ffn_norm_w'], 'L0_ffn_gate_w': _L0_ffn_in['gate_w'], 'L0_ffn_wg': _L0_ffn_in['wg'], 'L0_ffn_wu': _L0_ffn_in['wu'], 'L0_ffn_wd': _L0_ffn_in['wd'], 'L1_ffn_w_gate': _L1_ffn_in['w_gate'], 'L1_ffn_w_up': _L1_ffn_in['w_up'], 'L1_ffn_w_down': _L1_ffn_in['w_down'], 'L1_ffn_subln_weight': _L1_ffn_in['subln_weight'], 'L2_xattn_q_w': _L2_xattn_in['q_w'], 'L2_xattn_q_b': _L2_xattn_in['q_b'], 'L2_xattn_k_w': _L2_xattn_in['k_w'], 'L2_xattn_k_b': _L2_xattn_in['k_b'], 'L2_xattn_v_w': _L2_xattn_in['v_w'], 'L2_xattn_v_b': _L2_xattn_in['v_b'], 'L2_xattn_k_img_w': _L2_xattn_in['k_img_w'], 'L2_xattn_k_img_b': _L2_xattn_in['k_img_b'], 'L2_xattn_v_img_w': _L2_xattn_in['v_img_w'], 'L2_xattn_v_img_b': _L2_xattn_in['v_img_b'], 'L2_xattn_o_w': _L2_xattn_in['o_w'], 'L2_xattn_o_b': _L2_xattn_in['o_b'], 'L2_xattn_norm_q_w': _L2_xattn_in['norm_q_w'], 'L2_xattn_norm_k_w': _L2_xattn_in['norm_k_w'], 'L2_xattn_norm_k_img_w': _L2_xattn_in['norm_k_img_w'], 'L2_ffn_A': _L2_ffn_in['A'], 'L2_ffn_B': _L2_ffn_in['B'], 'L2_ffn_W': _L2_ffn_in['W'], 'L2_ffn_bias': _L2_ffn_in['bias'], 'L3_xattn_Wq': _L3_xattn_in['Wq'], 'L3_xattn_bq': _L3_xattn_in['bq'], 'L3_xattn_Wkv': _L3_xattn_in['Wkv'], 'L3_xattn_bkv': _L3_xattn_in['bkv'], 'L3_xattn_Wp': _L3_xattn_in['Wp'], 'L3_xattn_bp': _L3_xattn_in['bp'], 'L3_ffn_gate_w': _L3_ffn_in['gate_w'], 'L3_ffn_expert_gate': _L3_ffn_in['expert_gate'], 'L3_ffn_expert_up': _L3_ffn_in['expert_up'], 'L3_ffn_expert_down': _L3_ffn_in['expert_down'], 'L3_ffn_shared_gate': _L3_ffn_in['shared_gate'], 'L3_ffn_shared_up': _L3_ffn_in['shared_up'], 'L3_ffn_shared_down': _L3_ffn_in['shared_down']}

def reference(x, ctx_2048, mask_BxS2_bk0, L0_xattn_wq, L0_xattn_bq, L0_xattn_wkv, L0_xattn_bkv, L0_xattn_wp, L0_xattn_bp, L0_ffn_attn_norm_w, L0_ffn_q_w, L0_ffn_k_w, L0_ffn_v_w, L0_ffn_o_w, L0_ffn_q_norm_w, L0_ffn_k_norm_w, L0_ffn_ffn_norm_w, L0_ffn_gate_w, L0_ffn_wg, L0_ffn_wu, L0_ffn_wd, L1_ffn_w_gate, L1_ffn_w_up, L1_ffn_w_down, L1_ffn_subln_weight, L2_xattn_q_w, L2_xattn_q_b, L2_xattn_k_w, L2_xattn_k_b, L2_xattn_v_w, L2_xattn_v_b, L2_xattn_k_img_w, L2_xattn_k_img_b, L2_xattn_v_img_w, L2_xattn_v_img_b, L2_xattn_o_w, L2_xattn_o_b, L2_xattn_norm_q_w, L2_xattn_norm_k_w, L2_xattn_norm_k_img_w, L2_ffn_A, L2_ffn_B, L2_ffn_W, L2_ffn_bias, L3_xattn_Wq, L3_xattn_bq, L3_xattn_Wkv, L3_xattn_bkv, L3_xattn_Wp, L3_xattn_bp, L3_ffn_gate_w, L3_ffn_expert_gate, L3_ffn_expert_up, L3_ffn_expert_down, L3_ffn_shared_gate, L3_ffn_shared_up, L3_ffn_shared_down):
    import jax
    import jax.numpy as jnp

    def _L0_xattn_ref(x, cond, wq, bq, wkv, bkv, wp, bp):
        import jax, jax.numpy as jnp
        import numpy as np
        NUM_HEADS = 16

        def _qdq(x):
            s = jnp.maximum(jnp.max(jnp.abs(x), axis=-1, keepdims=True) / 127.0, 1e-08)
            return jnp.clip(jnp.round(x / s), -127.0, 127.0) * s
        B, N, C = x.shape
        M = cond.shape[1]
        H = NUM_HEADS
        Dh = C // H
        q = _qdq(x) @ _qdq(wq).T + bq
        kv = cond @ wkv.T + bkv
        k, v = jnp.split(kv, 2, axis=-1)
        q = q.reshape(B, N, H, Dh)
        k = k.reshape(B, M, H, Dh)
        v = v.reshape(B, M, H, Dh)
        scale = 1.0 / np.sqrt(Dh)
        attn = jax.nn.softmax(jnp.einsum('bnhd,bmhd->bhnm', q, k) * scale, axis=-1)
        o = jnp.einsum('bhnm,bmhd->bnhd', attn, v).reshape(B, N, C)
        out = _qdq(o) @ _qdq(wp).T + bp
        return out

    def _L0_ffn_ref(hidden, attn_norm_w, q_w, k_w, v_w, o_w, q_norm_w, k_norm_w, ffn_norm_w, gate_w, wg, wu, wd):
        import jax, jax.numpy as jnp
        import numpy as np
        ROPE_THETA = 1000000.0
        TOP_K = 2

        def rmsnorm(x, w, eps=1e-06):
            xf = x.astype(jnp.float32)
            n = jax.lax.rsqrt(jnp.mean(xf * xf, axis=-1, keepdims=True) + eps)
            return (xf * n).astype(x.dtype) * w

        def rope_tables(seq_len, head_dim):
            freqs = 1.0 / ROPE_THETA ** (jnp.arange(0, head_dim, 2, dtype=jnp.float32) / head_dim)
            t = jnp.arange(seq_len, dtype=jnp.float32)
            f = jnp.outer(t, freqs)
            return (jnp.cos(f), jnp.sin(f))

        def apply_rope(x, cos, sin):
            half = x.shape[-1] // 2
            x1, x2 = (x[..., :half], x[..., half:])
            c = cos[None, None]
            s = sin[None, None]
            return jnp.concatenate([x1 * c - x2 * s, x2 * c + x1 * s], axis=-1)
        B, S, D = hidden.shape
        hd = q_norm_w.shape[0]
        Hq = q_w.shape[0] // hd
        Hkv = k_w.shape[0] // hd
        n_rep = Hq // Hkv
        h = rmsnorm(hidden, attn_norm_w)
        q = (h @ q_w.T).reshape(B, S, Hq, hd)
        k = (h @ k_w.T).reshape(B, S, Hkv, hd)
        v = (h @ v_w.T).reshape(B, S, Hkv, hd)
        q = rmsnorm(q, q_norm_w).transpose(0, 2, 1, 3)
        k = rmsnorm(k, k_norm_w).transpose(0, 2, 1, 3)
        v = v.transpose(0, 2, 1, 3)
        cos, sin = rope_tables(S, hd)
        q = apply_rope(q, cos, sin)
        k = apply_rope(k, cos, sin)
        k = jnp.repeat(k, n_rep, axis=1)
        v = jnp.repeat(v, n_rep, axis=1)
        scale = 1.0 / jnp.sqrt(jnp.float32(hd))
        scores = jnp.einsum('bhqd,bhkd->bhqk', q, k) * scale
        causal = jnp.tril(jnp.ones((S, S), bool))
        scores = jnp.where(causal[None, None], scores, jnp.finfo(scores.dtype).min)
        attn = jnp.einsum('bhqk,bhkd->bhqd', jax.nn.softmax(scores, axis=-1), v)
        attn = attn.transpose(0, 2, 1, 3).reshape(B, S, Hq * hd)
        hidden = hidden + attn @ o_w.T
        h2 = rmsnorm(hidden, ffn_norm_w)
        T = B * S
        E = gate_w.shape[0]
        tok = h2.reshape(T, D)
        probs = jax.nn.softmax(tok @ gate_w.T, axis=-1)
        topv, topi = jax.lax.top_k(probs, TOP_K)
        topw = topv / (jnp.sum(topv, axis=-1, keepdims=True) + 1e-09)
        combine = jnp.zeros((T, E), tok.dtype).at[jnp.arange(T)[:, None], topi].set(topw)
        eg = jnp.einsum('td,eid->eti', tok, wg)
        eu = jnp.einsum('td,eid->eti', tok, wu)
        eo = jnp.einsum('eti,edi->etd', jax.nn.silu(eg) * eu, wd)
        moe_out = jnp.einsum('te,etd->td', combine, eo).reshape(B, S, D)
        return hidden + moe_out

    def _L1_xattn_ref(hidden_states, memory_tokens, memory_mask):
        import jax, jax.numpy as jnp
        import numpy as np
        B, S, D = hidden_states.shape
        scale = 1.0 / jnp.sqrt(jnp.asarray(D, hidden_states.dtype))
        scores = jnp.einsum('bsd,bmd->bsm', hidden_states, memory_tokens) * scale
        neg_inf = jnp.asarray(-1e+30, scores.dtype)
        scores = jnp.where(memory_mask[:, None, :], scores, neg_inf)
        attn = jax.nn.softmax(scores, axis=-1)
        readout = jnp.einsum('bsm,bmd->bsd', attn, memory_tokens)
        valid_b = jnp.any(memory_mask, axis=-1)
        out = jnp.where(valid_b[:, None, None], readout, jnp.zeros_like(readout))
        return out

    def _L1_ffn_ref(x, w_gate, w_up, w_down, subln_weight):
        import jax, jax.numpy as jnp
        import numpy as np
        EPS = 1e-05
        LN_EPS = 1e-06

        def activation_quant(x):
            scale = 127.0 / jnp.clip(jnp.max(jnp.abs(x), axis=-1, keepdims=True), EPS, None)
            return jnp.clip(jnp.round(x * scale), -128.0, 127.0) / scale

        def weight_quant(w):
            scale = 1.0 / jnp.clip(jnp.mean(jnp.abs(w)), EPS, None)
            return jnp.clip(jnp.round(w * scale), -1.0, 1.0) / scale

        def bit_linear(x, w):
            xq = x + jax.lax.stop_gradient(activation_quant(x) - x)
            wq = w + jax.lax.stop_gradient(weight_quant(w) - w)
            return jnp.einsum('bsh,oh->bso', xq, wq)

        def subln(x, g):
            var = jnp.mean(jnp.square(x), axis=-1, keepdims=True)
            return x * jax.lax.rsqrt(var + LN_EPS) * g
        gate = bit_linear(x, w_gate)
        up = bit_linear(x, w_up)
        activated = up * jnp.square(jax.nn.relu(gate))
        activated = subln(activated, subln_weight)
        return bit_linear(activated, w_down)

    def _L2_xattn_ref(x, context, q_w, q_b, k_w, k_b, v_w, v_b, k_img_w, k_img_b, v_img_w, v_img_b, o_w, o_b, norm_q_w, norm_k_w, norm_k_img_w):
        import jax, jax.numpy as jnp
        import numpy as np
        DIM = 256
        NH = 16
        HD = DIM // NH
        EPS = 1e-06
        IMG_LEN = 257

        def rms_norm(x, w, eps=EPS):
            xf = x.astype(jnp.float32)
            y = xf * jax.lax.rsqrt(jnp.mean(xf * xf, axis=-1, keepdims=True) + eps)
            return y.astype(x.dtype) * w

        def linear(x, w, b):
            return jnp.einsum('blc,oc->blo', x, w) + b

        def attention(q, k, v):
            scale = 1.0 / jnp.sqrt(jnp.asarray(HD, q.dtype))
            scores = jnp.einsum('bqhd,bkhd->bhqk', q, k) * scale
            probs = jax.nn.softmax(scores, axis=-1)
            return jnp.einsum('bhqk,bkhd->bqhd', probs, v)
        B, L, _ = x.shape
        ctx_img = context[:, :IMG_LEN]
        ctx_txt = context[:, IMG_LEN:]
        q = rms_norm(linear(x, q_w, q_b), norm_q_w).reshape(B, L, NH, HD)
        k = rms_norm(linear(ctx_txt, k_w, k_b), norm_k_w).reshape(B, -1, NH, HD)
        v = linear(ctx_txt, v_w, v_b).reshape(B, -1, NH, HD)
        k_img = rms_norm(linear(ctx_img, k_img_w, k_img_b), norm_k_img_w).reshape(B, -1, NH, HD)
        v_img = linear(ctx_img, v_img_w, v_img_b).reshape(B, -1, NH, HD)
        img_x = attention(q, k_img, v_img)
        txt_x = attention(q, k, v)
        out = (txt_x + img_x).reshape(B, L, DIM)
        return linear(out, o_w, o_b)

    def _L2_ffn_ref(x, A, B, W, bias):
        import jax, jax.numpy as jnp
        import numpy as np
        TOPK = 4
        vecs = jnp.einsum('arh,bsh->bsar', A, x)
        arrows = jnp.linalg.norm(vecs, axis=-1)
        _, idx = jax.lax.top_k(arrows, TOPK)
        routes = jax.nn.one_hot(idx, arrows.shape[-1], dtype=x.dtype).sum(-2) / TOPK
        v = jnp.einsum('bsa,bsar->bsr', routes, vecs)
        delta = jnp.einsum('bsa,ajr,bsr->bsj', routes, B, v)
        base = jnp.einsum('bsh,jh->bsj', x, W) + bias
        return base + delta

    def _L3_xattn_ref(x, cond, Wq, bq, Wkv, bkv, Wp, bp):
        import jax, jax.numpy as jnp
        import numpy as np
        D_MODEL = 256
        NUM_HEADS = 16
        HEAD_DIM = D_MODEL // NUM_HEADS

        def _fq_sym(x, axis):
            s = jnp.max(jnp.abs(x), axis=axis, keepdims=True) / 127.0
            s = jnp.maximum(s, 1e-08)
            q = jnp.clip(jnp.round(x / s), -127.0, 127.0) * s
            return x + jax.lax.stop_gradient(q - x)

        def _fq_unsigned(x, axis):
            s = jnp.max(x, axis=axis, keepdims=True) / 255.0
            s = jnp.maximum(s, 1e-08)
            q = jnp.clip(jnp.round(x / s), 0.0, 255.0) * s
            return x + jax.lax.stop_gradient(q - x)
        B, N, C = x.shape
        H, hd = (NUM_HEADS, HEAD_DIM)
        q = (x @ Wq + bq).reshape(1, B * N, H, hd)
        kv = (cond @ Wkv + bkv).reshape(1, -1, 2, H, hd)
        k, v = (kv[:, :, 0], kv[:, :, 1])
        scale = 1.0 / np.sqrt(hd).astype(np.float32)
        q = jnp.transpose(q * scale, (0, 2, 1, 3))
        k = jnp.transpose(k, (0, 2, 1, 3))
        v = jnp.transpose(v, (0, 2, 1, 3))
        q = _fq_sym(q, axis=-1)
        k = _fq_sym(k, axis=-1)
        v = _fq_sym(v, axis=2)
        attn = jnp.einsum('bhqd,bhkd->bhqk', q, k)
        attn = jax.nn.softmax(attn.astype(jnp.float32), axis=-1)
        attn = _fq_unsigned(attn, axis=-1)
        out = jnp.einsum('bhqk,bhkd->bhqd', attn, v)
        out = jnp.transpose(out, (0, 2, 1, 3)).reshape(B, N, C)
        return out @ Wp + bp

    def _L3_ffn_ref(hidden_states, gate_w, expert_gate, expert_up, expert_down, shared_gate, shared_up, shared_down):
        import jax, jax.numpy as jnp
        import numpy as np
        H = 256
        I = 176
        E = 8
        TOP_K = 2
        N_SHARED = 2
        I_SH = I * N_SHARED
        NORM_TOPK = True

        def _moe_forward(hidden_states, gate_w, expert_gate, expert_up, expert_down, shared_gate, shared_up, shared_down):
            bsz, seq_len, hdim = hidden_states.shape
            x = hidden_states.reshape(-1, hdim)
            logits = x @ gate_w.T
            probs = jax.nn.softmax(logits, axis=-1)
            routing_weights, selected = jax.lax.top_k(probs, TOP_K)
            if NORM_TOPK:
                routing_weights = routing_weights / (routing_weights.sum(axis=-1, keepdims=True) + 1e-20)
            combine = jnp.sum(jax.nn.one_hot(selected, E, dtype=routing_weights.dtype) * routing_weights[..., None], axis=1)
            g_sh = x @ shared_gate.T
            u_sh = x @ shared_up.T
            out = jax.nn.silu(g_sh) * u_sh @ shared_down.T
            g = jnp.einsum('nh,eih->nei', x, expert_gate)
            u = jnp.einsum('nh,eih->nei', x, expert_up)
            y = jnp.einsum('nei,ehi->neh', jax.nn.silu(g) * u, expert_down)
            out = out + jnp.einsum('neh,ne->nh', y, combine)
            return out.reshape(bsz, seq_len, hdim)
        return _moe_forward(hidden_states, gate_w, expert_gate, expert_up, expert_down, shared_gate, shared_up, shared_down)
    x = x + _L0_xattn_ref(_layernorm(x, axis=-1), ctx_2048, L0_xattn_wq, L0_xattn_bq, L0_xattn_wkv, L0_xattn_bkv, L0_xattn_wp, L0_xattn_bp)
    x = x + _L0_ffn_ref(_layernorm(x, axis=-1), L0_ffn_attn_norm_w, L0_ffn_q_w, L0_ffn_k_w, L0_ffn_v_w, L0_ffn_o_w, L0_ffn_q_norm_w, L0_ffn_k_norm_w, L0_ffn_ffn_norm_w, L0_ffn_gate_w, L0_ffn_wg, L0_ffn_wu, L0_ffn_wd)
    x = x + _L1_xattn_ref(_layernorm(x, axis=-1), ctx_2048, mask_BxS2_bk0)
    x = x + _L1_ffn_ref(_layernorm(x, axis=-1), L1_ffn_w_gate, L1_ffn_w_up, L1_ffn_w_down, L1_ffn_subln_weight)
    x = x + _L2_xattn_ref(_layernorm(x, axis=-1), ctx_2048, L2_xattn_q_w, L2_xattn_q_b, L2_xattn_k_w, L2_xattn_k_b, L2_xattn_v_w, L2_xattn_v_b, L2_xattn_k_img_w, L2_xattn_k_img_b, L2_xattn_v_img_w, L2_xattn_v_img_b, L2_xattn_o_w, L2_xattn_o_b, L2_xattn_norm_q_w, L2_xattn_norm_k_w, L2_xattn_norm_k_img_w)
    x = x + _L2_ffn_ref(_layernorm(x, axis=-1), L2_ffn_A, L2_ffn_B, L2_ffn_W, L2_ffn_bias)
    x = x + _L3_xattn_ref(_layernorm(x, axis=-1), ctx_2048, L3_xattn_Wq, L3_xattn_bq, L3_xattn_Wkv, L3_xattn_bkv, L3_xattn_Wp, L3_xattn_bp)
    x = x + _L3_ffn_ref(_layernorm(x, axis=-1), L3_ffn_gate_w, L3_ffn_expert_gate, L3_ffn_expert_up, L3_ffn_expert_down, L3_ffn_shared_gate, L3_ffn_shared_up, L3_ffn_shared_down)
    return x

_drawn_inputs = setup_inputs


def setup_inputs(seed=0):
    import zlib

    import numpy as np

    out = dict(_drawn_inputs(seed))
    spreads = {'L0_ffn_attn_norm_w': (1.0, 0.6),
     'L0_ffn_q_norm_w': (1.0, 0.6),
     'L0_ffn_k_norm_w': (1.0, 0.6),
     'L0_ffn_ffn_norm_w': (1.0, 0.6),
     'L1_ffn_subln_weight': (1.0, 0.6),
     'L2_xattn_q_b': (0.0, 2.0),
     'L2_xattn_k_b': (0.0, 0.1),
     'L2_xattn_v_b': (0.0, 0.1),
     'L2_xattn_k_img_b': (0.0, 2.0),
     'L2_xattn_v_img_b': (0.0, 0.539),
     'L2_xattn_o_b': (0.0, 0.314),
     'L2_xattn_norm_q_w': (1.0, 0.6),
     'L2_xattn_norm_k_w': (1.0, 0.2),
     'L2_xattn_norm_k_img_w': (1.0, 0.6),
     'L3_xattn_bq': (0.0, 0.8),
     'L3_xattn_bkv': (0.0, 0.62),
     'L3_xattn_bp': (0.0, 0.36)}
    factors = {'L0_xattn_wq': 8.0,
     'L0_xattn_bq': 8.0,
     'L0_xattn_bkv': 7.589,
     'L0_xattn_bp': 2.718,
     'L0_ffn_gate_w': 8.0,
     'L0_ffn_wg': 8.0,
     'L0_ffn_wu': 8.0,
     'L0_ffn_wd': 8.0,
     'L2_xattn_q_w': 39.563,
     'L2_xattn_k_img_w': 47.804,
     'L2_ffn_A': 8.0,
     'L2_ffn_B': 8.0,
     'L2_ffn_bias': 6.418,
     'L3_xattn_Wq': 8.0,
     'L3_xattn_Wkv': 8.0,
     'L3_xattn_Wp': 4.089,
     'L3_ffn_gate_w': 8.0,
     'L3_ffn_expert_gate': 8.0,
     'L3_ffn_expert_up': 8.0,
     'L3_ffn_expert_down': 8.0,
     'L3_ffn_shared_gate': 6.357,
     'L3_ffn_shared_up': 6.274,
     'L3_ffn_shared_down': 6.276,
     'L2_xattn_v_img_w': 4.096}
    for name, (base, spread) in spreads.items():
        noise = np.random.default_rng([zlib.crc32(name.encode()), seed]).standard_normal(out[name].shape)
        drawn = base * np.exp(spread * noise) if base else spread * noise
        out[name] = jnp.asarray(drawn.astype(out[name].dtype))
    for name, factor in factors.items():
        out[name] = (out[name] * factor).astype(out[name].dtype)
    return out
```

```python
from contextlib import ExitStack

import concourse.bass as bass
from concourse import mybir

F32 = mybir.dt.float32
BF16 = mybir.dt.bfloat16
U8 = mybir.dt.uint8
ALU = mybir.AluOpType
ACT = mybir.ActivationFunctionType
X = mybir.AxisListType.X
RMAX = bass.bass_isa.ReduceOp.max
RADD = bass.bass_isa.ReduceOp.add

P = 128
B = 16
D = 256
DC = D // P
NH, HD = 16, 16
GH, GKV, GD = 16, 4, 128
E, I, ISH = 8, 176, 352
EI = E * I
F = 1024
AR, RR = 64, 16
PAIR = 2
NI = B // PAIR
MAGIC = 12582912.0
NEG = -1.0e30

W_XATT0 = dict(wq=DC * D, wp=DC * D, wk=DC * 2 * D, wv=DC * D, bq=4, bk=4, bv=D, bp=D)
W_GQA = dict(wq=DC * GH * GD, wk=DC * GKV * GD, wv=DC * GKV * GD, wo=GH * D, norm=D,
             qn=GD, kn=GD, cos=GD // 2, sin=GD // 2)
W_MOE0 = dict(gate=DC * E, wg=DC * EI, wu=DC * EI, wd=EI // P * D, norm=D)
W_BIT = dict(wg=DC * F, wu=DC * F, wd=F // P * D, g=F)
W_XATT2 = dict(wq=DC * D, wk=DC * D, wv=DC * D, wo=DC * D, bq=D, bk=D, bv=D, bo=D, nq=D, nk=D)
W_ARROW = dict(a=DC * AR * RR, b=AR * RR // P * D, w=DC * D, bias=D)
W_QKV3 = dict(wq=DC * D, wk=DC * D, wv=DC * D, bq=D, bk=D, bv=D)
GU3 = EI + ISH
DN3 = -(-GU3 // P)
W_MOE3 = dict(wp=DC * D, bp=D, gate=DC * E, wg=DC * GU3, wu=DC * GU3, wd=DN3 * D)


def words(layout):
    return sum(layout.values())


def part(arena, layout, name):
    names = list(layout)
    at = sum(layout[k] for k in names[:names.index(name)])
    return arena[:, at:at + layout[name]]


def semaphores(nc, ctx, phase, names):
    return {k: ctx.enter_context(nc.semaphore(phase + k)) for k in names.split()}


def end_phase(nc, sems):
    numbers = sorted(s.num for s in sems.values())
    nc.all_engine_barrier()
    nc.gpsimd.sem_clear(range(numbers[0], numbers[-1] + 1))
    nc.all_engine_barrier()


def tiles(eng, t):
    n = [t * PAIR + (j + 1) for j in range(PAIR)]
    return n if isinstance(t, int) else [eng.snap(x) for x in n]


def overlapped(eng, body):
    body(0, None)
    with eng.Fori(1, NI) as i:
        body(i, eng.snap(i - 1))
    body(None, NI - 1)


def halves(eng, front, back):
    def half(t):
        n = tiles(eng, t) if t is not None else None

        def run(stage, *js):
            if t is not None:
                for j in js:
                    stage(j, n, t + 1)
        return run
    return half(front), half(back)


def loads_ahead(sp, load, store, start_next):
    load(0)
    load(1)
    start_next()
    with sp.Fori(2, NI) as i:
        load(i)
        store(sp.snap(i - 2))
    store(NI - 2)
    store(NI - 1)


def hold(dve, scratch, sem, value):
    dve.wait_ge(sem, value)
    dve.memset(scratch, 0.0)


def credit(nc, k, sems, **first):
    for c, (name, count) in enumerate(first.items()):
        nc.vector.memset(k["scratch"][:, 8 + c:9 + c], 0.0).then_inc(sems[name], count)


def xatt0(nc, k, x_in, x_out, ctx_T, arena, load_next):
    with ExitStack() as ctx:
        def sb(name, shape, dt=F32):
            return ctx.enter_context(nc.sbuf_tensor("xatt0_" + name, shape, dt))

        def w(name):
            return part(arena, W_XATT0, name)

        ready = k["ready"]
        s = semaphores(nc, ctx, "xatt0_", """
            wmax wscale wrecip wround wq_int wt_psum wt_done weights_next
            x_loaded0 x_loaded1 c_loaded0 c_loaded1 stored0 stored1 stats mean var rstd normed amax scale recip rounded quantised kept
            kT_psum kT v_psum v biased xT_psum xT qT_psum qT s_psum row_max shifted exped
            pT_psum pT o_psum denom o_norm o_amax o_scale o_recip o_rounded o_quantised oT_psum oT
            y_psum y""")
        S = k["psum"][:, 0:4, :].rearrange("p g (c m) -> p g c m", c=4)
        TP = k["psum"][:, 4:6, :].rearrange("p r (c m) -> p r c m", c=4)
        V = k["psum"][:, 4:6, :]
        M = k["psum"][:, 6:8, :]
        wsm = sb("wsm", [P, 2 * DC, 3])
        wi = sb("wi", [P, 2 * DC, D])
        wqT = sb("wqT", [P, DC, NH, 32])
        wpT = sb("wpT", [P, DC, D])
        one = sb("one", [P, 1])
        xt = sb("xt", [P, PAIR, D])
        ct = sb("ct", [P, PAIR, DC, P])
        st = sb("st", [P, PAIR, 6])
        mv = sb("mv", [P, PAIR, 2])
        sm = sb("sm", [P, PAIR, 8])
        xn = sb("xn", [P, PAIR, D])
        xb = sb("xb", [P, PAIR, D])
        xr = sb("xr", [P, PAIR, D])
        xT = sb("xT", [P, PAIR, DC, P])
        qT = sb("qT", [P, PAIR, 4, P])
        kT = sb("kT", [P, PAIR, 4, P])
        v = sb("v", [P, PAIR, NH, HD + 1])
        mx = sb("mx", [P, PAIR, 4, 4])
        pr = sb("pr", [P, PAIR, 4, 4, P])
        pT = sb("pT", [P, PAIR, 4, 4, P])
        rd = sb("rd", [P, PAIR, NH])
        o = sb("o", [P, PAIR, D])
        oT = sb("oT", [P, PAIR, DC, P])
        y = sb("y", [P, PAIR, D])
        block = ctx.enter_context(nc.Block())

        @block.sync
        def _(sp):
            def load(t):
                for j in range(PAIR):
                    sp.wait_ge(s["v"], t * PAIR + 1)
                    sp.wait_ge(s["biased"], t * PAIR + 1)
                    sp.dma_start(ct[:, j], ctx_T[t * PAIR + j]).then_inc(s[f"c_loaded{j}"], 16)
                    sp.dma_start(xt[:, j], x_in[t * PAIR + j]).then_inc(s[f"x_loaded{j}"], 16)

            def store(t):
                m = tiles(sp, t)
                for j in range(PAIR):
                    sp.wait_ge(s["y"], m[j] + 1)
                    sp.dma_start(x_out[t * PAIR + j], y[:, j]).then_inc(s[f"stored{j}"], 16)

            start_next, finish_next = load_next
            loads_ahead(sp, load, store, lambda: start_next(sp, s["weights_next"]))
            for j in range(PAIR):
                sp.wait_ge(s[f"stored{j}"], (NI + 1) * 16)
            finish_next(sp, s["weights_next"])

        @block.gpsimd
        def _(pool):
            nc.gpsimd.memset(wqT[:], 0.0)
            nc.gpsimd.memset(v[:], 1.0).then_inc(s["wt_done"], 1)
            nc.gpsimd.memset(one[:], 1.0).then_inc(s["wt_done"], 1)

            def body(front, back):
                if front is not None:
                    n, turn = tiles(pool, front), front + 1
                    for j in range(PAIR):
                        pool.wait_ge(s["var"], n[j])
                        nc.gpsimd.tensor_tensor(sm[:, j, 1:2], sm[:, j, 0:1], k["neg_half"][:], ALU.pow).then_inc(s["rstd"], 1)
                    for j in range(PAIR):
                        pool.wait_ge(s[f"x_loaded{j}"], turn * 16)
                        pool.wait_ge(s["kept"], n[j])
                        nc.gpsimd.tensor_tensor(xb[:, j], xt[:, j], w("bp"), ALU.add).then_inc(s["biased"], 1)
                    for j in range(PAIR):
                        if back is not None:
                            pool.wait_ge(s["y"], n[j] - 1)
                        pool.wait_ge(s["biased"], n[j] + 1)
                        nc.gpsimd.tensor_tensor(xr[:, j], xb[:, j], one[:].to_broadcast([P, D]), ALU.mult).then_inc(s["kept"], 1)

            overlapped(pool, body)

        @block.scalar
        def _(act):
            def turned_x(j, n, t):
                act.wait_ge(s["xT_psum"], n[j])
                nc.scalar.copy(xT[:, j], M[:, j, 0:DC * P]).then_inc(s["xT"], 1)

            def exp(j, n, t):
                act.wait_ge(s["shifted"], n[j] + 1)
                nc.scalar.activation(pr[:, j], pr[:, j], ACT.Exp, scale=HD ** -0.5).then_inc(s["exped"], 1)

            def turned_p(j, n, t):
                for g in range(4):
                    act.wait_ge(s["pT_psum"], n[j] * 4 + (g - 3))
                    nc.scalar.copy(pT[:, j, g], TP[:, g % 2]).then_inc(s["pT"], 1)

            def turned_o(j, n, t):
                act.wait_ge(s["oT_psum"], n[j])
                nc.scalar.copy(oT[:, j], M[:, j, 0:DC * P]).then_inc(s["oT"], 1)

            def body(front, back):
                f, b = halves(act, front, back)
                for j in range(PAIR):
                    b(exp, j)
                    f(turned_x, j)
                    b(turned_p, j)
                b(turned_o, 0, 1)

            overlapped(act, body)

        @block.vector
        def _(dve):
            credit(nc, k, s, y=1, v=1, biased=1, kept=2, shifted=1, pT=1, stored0=16, stored1=16)
            for m, name in enumerate(("wq", "wp")):
                nc.vector.tensor_reduce(wsm[:, m * DC:(m + 1) * DC, 0], w(name).rearrange("p (c d) -> p c d", c=DC),
                                        X, ALU.max, apply_absolute_value=True).then_inc(s["wmax"], 1)
            dve.wait_ge(s["wmax"], 2)
            nc.vector.tensor_scalar(wsm[:, :, 1], wsm[:, :, 0], 1.0 / 127.0, 1e-8, ALU.mult, ALU.max).then_inc(s["wscale"], 1)
            dve.wait_ge(s["wscale"], 1)
            nc.vector.reciprocal(wsm[:, :, 2], wsm[:, :, 1]).then_inc(s["wrecip"], 1)
            dve.wait_ge(s["wrecip"], 1)
            for c in range(2 * DC):
                src = w("wq" if c < DC else "wp").rearrange("p (c d) -> p c d", c=DC)[:, c % DC]
                nc.vector.tensor_scalar(wi[:, c], src, wsm[:, c, 2:3], MAGIC, ALU.mult, ALU.add).then_inc(s["wround"], 1)
            for c in range(2 * DC):
                dve.wait_ge(s["wround"], c + 1)
                nc.vector.tensor_scalar(wi[:, c], wi[:, c], MAGIC, wsm[:, c, 1:2], ALU.subtract, ALU.mult).then_inc(s["wq_int"], 1)
            dve.wait_ge(s["wt_done"], 2)
            dve.wait_ge(s["wt_psum"], 1)
            for ic in range(DC):
                for oc in range(DC):
                    nc.vector.tensor_copy(wqT[:, ic, 8 * oc:8 * oc + 8, 0:HD],
                                          TP[:, 0, oc * DC + ic].rearrange("p (h d) -> p h d", d=HD))
                    last = nc.vector.tensor_copy(wpT[:, ic, oc * P:(oc + 1) * P], TP[:, 1, oc * DC + ic])
            last.then_inc(s["wt_done"], 1)

            def norm(j, n, turn):
                dve.wait_ge(s[f"x_loaded{j}"], turn * 16)
                nc.vector.bn_stats(st[:, j], xt[:, j]).then_inc(s["stats"], 1)
                hold(dve, k["scratch"][:, j:j + 1], s["stats"], n[j])
                nc.vector.bn_aggr(mv[:, j], st[:, j]).then_inc(s["mean"], 1)
                dve.wait_ge(s["mean"], n[j])
                nc.vector.tensor_scalar(sm[:, j, 0:1], mv[:, j, 1:2], 1e-5, None, ALU.add).then_inc(s["var"], 1)

            def quantise(j, n, turn):
                dve.wait_ge(s["rstd"], n[j])
                nc.vector.tensor_scalar(xn[:, j], xt[:, j], mv[:, j, 0:1], sm[:, j, 1:2], ALU.subtract, ALU.mult).then_inc(s["normed"], 1)
                dve.wait_ge(s["normed"], n[j])
                nc.vector.tensor_reduce(sm[:, j, 2:3], xn[:, j], X, ALU.max, apply_absolute_value=True).then_inc(s["amax"], 1)
                dve.wait_ge(s["amax"], n[j])
                nc.vector.tensor_scalar(sm[:, j, 3:4], sm[:, j, 2:3], 1.0 / 127.0, 1e-8, ALU.mult, ALU.max).then_inc(s["scale"], 1)
                dve.wait_ge(s["scale"], n[j])
                nc.vector.reciprocal(sm[:, j, 4:5], sm[:, j, 3:4]).then_inc(s["recip"], 1)
                dve.wait_ge(s["recip"], n[j])
                nc.vector.tensor_scalar(xn[:, j], xn[:, j], sm[:, j, 4:5], MAGIC, ALU.mult, ALU.add).then_inc(s["rounded"], 1)
                dve.wait_ge(s["rounded"], n[j])
                nc.vector.tensor_scalar(xn[:, j], xn[:, j], MAGIC, sm[:, j, 3:4], ALU.subtract, ALU.mult).then_inc(s["quantised"], 1)

            def keys(j, n, turn):
                dve.wait_ge(s["kT_psum"], n[j])
                nc.vector.tensor_tensor(kT[:, j], M[:, j].rearrange("p (c m) -> p c m", c=4),
                                        w("bk").unsqueeze(2).to_broadcast([P, 4, P]), ALU.add).then_inc(s["kT"], 1)

            def values(j, n, turn):
                dve.wait_ge(s["v_psum"], n[j])
                nc.vector.tensor_tensor(v[:, j, :, 0:HD], V[:, j, 0:D].rearrange("p (h d) -> p h d", d=HD),
                                        w("bv").rearrange("p (h d) -> p h d", d=HD), ALU.add).then_inc(s["v"], 1)

            def queries(j, n, turn):
                dve.wait_ge(s["qT_psum"], n[j])
                nc.vector.tensor_tensor(qT[:, j], V[:, j].rearrange("p (c m) -> p c m", c=4),
                                        w("bq").unsqueeze(2).to_broadcast([P, 4, P]), ALU.add).then_inc(s["qT"], 1)

            def softmax(j, n, turn):
                dve.wait_ge(s["s_psum"], n[j])
                nc.vector.tensor_reduce(mx[:, j], S, X, ALU.max).then_inc(s["row_max"], 1)
                dve.wait_ge(s["row_max"], n[j])
                for g in range(4):
                    last = nc.vector.tensor_tensor(pr[:, j, g], S[:, g], mx[:, j, g].unsqueeze(2).to_broadcast([P, 4, P]), ALU.subtract)
                last.then_inc(s["shifted"], 1)

            def output(j, n, turn):
                O = M[:, j, 0:NH * (HD + 1)].rearrange("p (h d) -> p h d", h=NH)
                dve.wait_ge(s["o_psum"], n[j])
                nc.vector.reciprocal(rd[:, j], O[:, :, HD]).then_inc(s["denom"], 1)
                dve.wait_ge(s["denom"], n[j])
                nc.vector.tensor_tensor(o[:, j].rearrange("p (h d) -> p h d", h=NH), O[:, :, 0:HD],
                                        rd[:, j].unsqueeze(2).to_broadcast([P, NH, HD]), ALU.mult).then_inc(s["o_norm"], 1)
                dve.wait_ge(s["o_norm"], n[j])
                nc.vector.tensor_reduce(sm[:, j, 5:6], o[:, j], X, ALU.max, apply_absolute_value=True).then_inc(s["o_amax"], 1)
                dve.wait_ge(s["o_amax"], n[j])
                nc.vector.tensor_scalar(sm[:, j, 6:7], sm[:, j, 5:6], 1.0 / 127.0, 1e-8, ALU.mult, ALU.max).then_inc(s["o_scale"], 1)
                dve.wait_ge(s["o_scale"], n[j])
                nc.vector.reciprocal(sm[:, j, 7:8], sm[:, j, 6:7]).then_inc(s["o_recip"], 1)
                dve.wait_ge(s["o_recip"], n[j])
                nc.vector.tensor_scalar(o[:, j], o[:, j], sm[:, j, 7:8], MAGIC, ALU.mult, ALU.add).then_inc(s["o_rounded"], 1)
                dve.wait_ge(s["o_rounded"], n[j])
                nc.vector.tensor_scalar(o[:, j], o[:, j], MAGIC, sm[:, j, 6:7], ALU.subtract, ALU.mult).then_inc(s["o_quantised"], 1)

            def residual(j, n, turn):
                dve.wait_ge(s["y_psum"], n[j])
                dve.wait_ge(s["kept"], n[j] + 2)
                dve.wait_ge(s[f"stored{j}"], turn * 16)
                nc.vector.tensor_tensor(y[:, j], M[:, j, 0:D], xr[:, j], ALU.add).then_inc(s["y"], 1)

            def body(front, back):
                f, b = halves(dve, front, back)
                f(norm, 0, 1)
                b(softmax, 0)
                f(keys, 0)
                f(quantise, 0, 1)
                b(softmax, 1)
                f(keys, 1)
                b(output, 0)
                f(values, 0, 1)
                b(output, 1)
                f(queries, 0, 1)
                b(residual, 0, 1)

            overlapped(dve, body)

        @block.tensor
        def _(pe):
            pe.wait_ge(s["wq_int"], 2 * DC)
            for m in range(2):
                for oc in range(DC):
                    for ic in range(DC):
                        last = nc.tensor.transpose(TP[:, m, oc * DC + ic], wi[:, m * DC + oc, ic * P:(ic + 1) * P], k["ident"][:])
            last.then_inc(s["wt_psum"], 1)
            pe.wait_ge(s["wt_done"], 3)

            def keys(j, n, turn):
                pe.wait_ge(s[f"c_loaded{j}"], turn * 16)
                wk = w("wk").rearrange("p (c o) -> p c o", c=DC)
                for c in range(4):
                    for ic in range(DC):
                        last = nc.tensor.matmul(M[:, j, c * P:(c + 1) * P], wk[:, ic, c * P:(c + 1) * P], ct[:, j, ic],
                                                start=ic == 0, stop=ic == DC - 1)
                last.then_inc(s["kT_psum"], 1)

            def values(j, n, turn):
                wv = w("wv").rearrange("p (c o) -> p c o", c=DC)
                for ic in range(DC):
                    last = nc.tensor.matmul(V[:, j, 0:D], ct[:, j, ic], wv[:, ic], start=ic == 0, stop=ic == DC - 1)
                last.then_inc(s["v_psum"], 1)

            def turn_x(j, n, turn):
                pe.wait_ge(s["quantised"], n[j])
                pe.wait_ge(s["kT"], n[j])
                for ic in range(DC):
                    last = nc.tensor.transpose(M[:, j, ic * P:(ic + 1) * P], xn[:, j, ic * P:(ic + 1) * P], k["ident"][:])
                last.then_inc(s["xT_psum"], 1)

            def queries(j, n, turn):
                pe.wait_ge(s["xT"], n[j])
                pe.wait_ge(s["v"], n[j] + 1)
                for c in range(4):
                    for ic in range(DC):
                        last = nc.tensor.matmul(V[:, j, c * P:(c + 1) * P],
                                                wqT[:, ic, 4 * c:4 * c + 4].rearrange("p h d -> p (h d)"), xT[:, j, ic],
                                                start=ic == 0, stop=ic == DC - 1)
                last.then_inc(s["qT_psum"], 1)

            def scores(j, n, turn):
                pe.wait_ge(s["qT"], n[j])
                pe.wait_ge(s["shifted"], n[j])
                for c in range(4):
                    for g in range(4):
                        r = slice(32 * g, 32 * g + 32)
                        last = nc.tensor.matmul(S[:, g, c], qT[r, j, c], kT[r, j, c], start=True, stop=True)
                last.then_inc(s["s_psum"], 1)

            def turn_p(j, n, turn):
                pe.wait_ge(s["exped"], n[j])
                for g in range(4):
                    if g < 2:
                        pe.wait_ge(s["pT"], n[j] * 4 - 3)
                    else:
                        pe.wait_ge(s["pT"], n[j] * 4 + (g - 4))
                    for c in range(4):
                        last = nc.tensor.transpose(TP[:, g % 2, c], pr[:, j, g, c], k["ident"][:])
                    last.then_inc(s["pT_psum"], 1)

            def attend(j, n, turn):
                O = M[:, j, 0:NH * (HD + 1)].rearrange("p (h d) -> p h d", h=NH)
                pe.wait_ge(s["pT"], n[j] * 4 + 1)
                for c in range(4):
                    for g in range(4):
                        last = nc.tensor.matmul(O[:, 4 * c + g], pT[:, j, g, c], v[:, j, 4 * c + g], start=True, stop=True)
                last.then_inc(s["o_psum"], 1)

            def turn_o(j, n, turn):
                pe.wait_ge(s["o_quantised"], n[j])
                for ic in range(DC):
                    last = nc.tensor.transpose(M[:, j, ic * P:(ic + 1) * P], o[:, j, ic * P:(ic + 1) * P], k["ident"][:])
                last.then_inc(s["oT_psum"], 1)

            def project(j, n, turn):
                pe.wait_ge(s["oT"], n[j])
                for ic in range(DC):
                    last = nc.tensor.matmul(M[:, j, 0:D], oT[:, j, ic], wpT[:, ic], start=ic == 0, stop=ic == DC - 1)
                last.then_inc(s["y_psum"], 1)

            def body(front, back):
                f, b = halves(pe, front, back)
                b(scores, 0)
                if back is not None:
                    pe.wait_ge(s["y"], back * PAIR + 1)
                f(keys, 0, 1)
                b(scores, 1)
                for j in range(PAIR):
                    f(turn_x, j)
                    b(turn_p, j)
                if front is not None:
                    pe.wait_ge(s["xT"], (front + 1) * PAIR)
                b(attend, 0, 1)
                f(values, 0, 1)
                f(queries, 0, 1)
                b(turn_o, 0, 1)
                b(project, 0, 1)

            overlapped(pe, body)
    end_phase(nc, s)


def gqa(nc, k, x_in, hid_out, arena, load_next):
    HQK = GH + GKV
    GROUPS = HQK // 4 + GH // 4
    SEQ = PAIR * GROUPS
    with ExitStack() as ctx:
        def sb(name, shape, dt=F32):
            return ctx.enter_context(nc.sbuf_tensor("gqa_" + name, shape, dt))

        def w(name):
            return part(arena, W_GQA, name)

        s = semaphores(nc, ctx, "gqa_", """
            mask_made tables weights_next x_loaded0 x_loaded1 stored0 stored1
            stats mean var rstd ms1 ms ms_eps rms normed scaled hT_psum hT k_psum k_copied v_psum v_copied
            q_psum q_copied squared summed q_eps q_rms rope_a rope_b roped qk_scaled
            turned evacuated s_psum row_max shifted exped row_sum row_recip p_norm oT_psum oT y_psum kept y""")
        BIG = k["psum"][:, 0:4, :]
        TP = k["psum"][:, 4:6, :].rearrange("p r (c m) -> p r c m", c=4)
        M = k["psum"][:, 6:8, :]
        rot = sb("rot", [P, 4, GD])
        cmask = sb("cmask", [P, 4, P], BF16)
        one = sb("one", [P, 1])
        xt = sb("xt", [P, PAIR, D])
        st = sb("st", [P, PAIR, 6])
        mv = sb("mv", [P, PAIR, 2])
        sm = sb("sm", [P, PAIR, 8])
        xn = sb("xn", [P, PAIR, D])
        xr = sb("xr", [P, PAIR, D])
        h = sb("h", [P, PAIR, D])
        hT = sb("hT", [P, PAIR, DC, P])
        v = sb("v", [P, PAIR, GKV, GD])
        qs = sb("qs", [P, PAIR, HQK, GD])
        ra = sb("ra", [P, PAIR, HQK, GD])
        rb = sb("rb", [P, HQK, GD])
        qkT = sb("qkT", [P, PAIR, HQK, P])
        pr = sb("pr", [P, PAIR, GH, P])
        pT = sb("pT", [P, PAIR, GH, P])
        nq = sb("nq", [P, PAIR, 2, HQK])
        mx = sb("mx", [P, PAIR, 3, GH])
        y = sb("y", [P, PAIR, D])
        block = ctx.enter_context(nc.Block())

        @block.sync
        def _(sp):
            def load(t):
                for j in range(PAIR):
                    sp.wait_ge(s["normed"], t * PAIR + 1)
                    sp.dma_start(xt[:, j], x_in[t * PAIR + j]).then_inc(s[f"x_loaded{j}"], 16)

            def store(t):
                m = tiles(sp, t)
                for j in range(PAIR):
                    sp.wait_ge(s["y"], m[j] + 1)
                    sp.dma_start(hid_out[t * PAIR + j], y[:, j]).then_inc(s[f"stored{j}"], 16)

            start_next, finish_next = load_next
            loads_ahead(sp, load, store, lambda: start_next(sp, s["weights_next"]))
            for j in range(PAIR):
                sp.wait_ge(s[f"stored{j}"], (NI + 1) * 16)
            finish_next(sp, s["weights_next"])

        @block.gpsimd
        def _(pool):
            nc.gpsimd.memset(one[:], 1.0)
            nc.gpsimd.memset(cmask[:], 0.0).then_inc(s["mask_made"], 1)
            pool.wait_ge(s["mask_made"], 1)
            nc.gpsimd.affine_select(out=cmask[:], in_=cmask[:], compare_op=ALU.is_ge, fill=NEG, base=0,
                                    pattern=[[0, 4], [-1, P]], channel_multiplier=1).then_inc(s["mask_made"], 1)

            def body(front, back):
                if front is not None:
                    n = tiles(pool, front)
                    for j in range(PAIR):
                        pool.wait_ge(s["var"], n[j])
                        nc.gpsimd.tensor_tensor(sm[:, j, 1:2], sm[:, j, 0:1], k["neg_half"][:], ALU.pow).then_inc(s["rstd"], 1)
                    for j in range(PAIR):
                        pool.wait_ge(s["ms_eps"], n[j])
                        nc.gpsimd.tensor_tensor(sm[:, j, 5:6], sm[:, j, 4:5], k["neg_half"][:], ALU.pow).then_inc(s["rms"], 1)
                    for j in range(PAIR):
                        pool.wait_ge(s["q_eps"], n[j])
                        nc.gpsimd.tensor_tensor(nq[:, j, 1], nq[:, j, 0], k["neg_half"][:].to_broadcast([P, HQK]), ALU.pow).then_inc(s["q_rms"], 1)
                        pool.wait_ge(s["roped"], n[j] + 1)
                        pool.wait_ge(s["q_rms"], n[j])
                        nc.gpsimd.tensor_tensor(ra[:, j], ra[:, j], nq[:, j, 1].unsqueeze(2).to_broadcast([P, HQK, GD]), ALU.mult).then_inc(s["qk_scaled"], 1)
                    for j in range(PAIR):
                        if back is not None:
                            pool.wait_ge(s["y"], n[j] - 1)
                        pool.wait_ge(s["normed"], n[j] + 1)
                        nc.gpsimd.tensor_tensor(xr[:, j], xn[:, j], one[:].to_broadcast([P, D]), ALU.mult).then_inc(s["kept"], 1)

            overlapped(pool, body)

        @block.scalar
        def _(act):
            def turned_h(j, n, t):
                act.wait_ge(s["hT_psum"], n[j])
                nc.scalar.copy(hT[:, j], M[:, j, 0:DC * P]).then_inc(s["hT"], 1)

            def keys(j, n, t):
                act.wait_ge(s["k_psum"], n[j])
                act.wait_ge(s["roped"], n[0])
                nc.scalar.copy(qs[:, j, GH:HQK], M[:, j]).then_inc(s["k_copied"], 1)

            def values(j, n, t, m):
                act.wait_ge(s["v_psum"], n[j])
                if m is not None:
                    act.wait_ge(s["oT_psum"], m[j])
                nc.scalar.copy(v[:, j], M[:, j]).then_inc(s["v_copied"], 1)

            def queries(j, n, t):
                act.wait_ge(s["q_psum"], n[j])
                nc.scalar.copy(qs[:, j, 0:GH], BIG).then_inc(s["q_copied"], 1)
                act.wait_ge(s["q_copied"], n[j])
                act.wait_ge(s["k_copied"], n[j])
                act.wait_ge(s["roped"], n[j])
                nc.scalar.activation(rb[:], qs[:, j], ACT.Square).then_inc(s["squared"], 1)

            def evacuate(buf, j, t, groups, first):
                for g in range(groups):
                    act.wait_ge(s["turned"], t * SEQ + (first + g + 1))
                    nc.scalar.copy(buf[:, j, 4 * g:4 * g + 4], TP[:, (first + g) % 2]).then_inc(s["evacuated"], 1)

            def turned_qk(j, n, t):
                evacuate(qkT, j, t, HQK // 4, j * (HQK // 4))

            def exp(j, n, t):
                act.wait_ge(s["shifted"], n[j])
                nc.scalar.activation(pr[:, j], pr[:, j], ACT.Exp, scale=GD ** -0.5).then_inc(s["exped"], 1)

            def turned_p(j, n, t):
                evacuate(pT, j, t, GH // 4, PAIR * (HQK // 4) + j * (GH // 4))

            def attended(j, n, t):
                act.wait_ge(s["oT_psum"], n[j])
                nc.scalar.copy(pr[:, j], BIG).then_inc(s["oT"], 1)

            def body(front, back):
                n = tiles(act, front) if front is not None else None
                m = tiles(act, back) if back is not None else None
                if back is not None:
                    turned_qk(0, m, back)
                if front is not None:
                    for stage in (turned_h, keys):
                        for j in range(PAIR):
                            stage(j, n, front)
                if back is not None:
                    turned_qk(1, m, back)
                    for j in range(PAIR):
                        exp(j, m, back)
                if front is not None:
                    queries(0, n, front)
                if back is not None:
                    for stage in (turned_p, attended):
                        for j in range(PAIR):
                            stage(j, m, back)
                if front is not None:
                    for j in range(PAIR):
                        values(j, n, front, m)
                    queries(1, n, front)

            overlapped(act, body)

        @block.vector
        def _(dve):
            credit(nc, k, s, y=1, oT=1, normed=1, roped=1, kept=2, evacuated=2, stored0=16, stored1=16)
            half = GD // 2
            cos, sin = w("cos"), w("sin")
            for m, name in enumerate(("qn", "kn")):
                wn = w(name)
                nc.vector.tensor_tensor(rot[:, 2 * m, 0:half], cos, wn[:, 0:half], ALU.mult)
                nc.vector.tensor_tensor(rot[:, 2 * m, half:], cos, wn[:, half:], ALU.mult)
                nc.vector.scalar_tensor_tensor(rot[:, 2 * m + 1, 0:half], sin, -1.0, wn[:, half:], ALU.mult, ALU.mult)
                last = nc.vector.tensor_tensor(rot[:, 2 * m + 1, half:], sin, wn[:, 0:half], ALU.mult)
            last.then_inc(s["tables"], 1)
            dve.wait_ge(s["tables"], 1)

            def norm(j, n, turn):
                dve.wait_ge(s[f"x_loaded{j}"], turn * 16)
                nc.vector.bn_stats(st[:, j], xt[:, j]).then_inc(s["stats"], 1)
                hold(dve, k["scratch"][:, j:j + 1], s["stats"], n[j])
                nc.vector.bn_aggr(mv[:, j], st[:, j]).then_inc(s["mean"], 1)
                dve.wait_ge(s["mean"], n[j])
                nc.vector.tensor_scalar(sm[:, j, 0:1], mv[:, j, 1:2], 1e-5, None, ALU.add).then_inc(s["var"], 1)

            def rms(j, n, turn):
                dve.wait_ge(s["rstd"], n[j])
                dve.wait_ge(s["kept"], n[j])
                nc.vector.tensor_scalar(xn[:, j], xt[:, j], mv[:, j, 0:1], sm[:, j, 1:2], ALU.subtract, ALU.mult).then_inc(s["normed"], 1)
                nc.vector.tensor_tensor(sm[:, j, 2:3], mv[:, j, 1:2], sm[:, j, 1:2], ALU.mult).then_inc(s["ms1"], 1)
                dve.wait_ge(s["ms1"], n[j])
                nc.vector.tensor_tensor(sm[:, j, 3:4], sm[:, j, 2:3], sm[:, j, 1:2], ALU.mult).then_inc(s["ms"], 1)
                dve.wait_ge(s["ms"], n[j])
                nc.vector.tensor_scalar(sm[:, j, 4:5], sm[:, j, 3:4], 1e-6, None, ALU.add).then_inc(s["ms_eps"], 1)

            def scale(j, n, turn):
                dve.wait_ge(s["rms"], n[j])
                dve.wait_ge(s["normed"], n[j] + 1)
                nc.vector.scalar_tensor_tensor(h[:, j], xn[:, j], sm[:, j, 5:6], w("norm"), ALU.mult, ALU.mult).then_inc(s["scaled"], 1)

            def rope(j, n, turn):
                dve.wait_ge(s["squared"], n[j])
                nc.vector.tensor_reduce(nq[:, j, 0], rb[:], X, ALU.add).then_inc(s["summed"], 1)
                dve.wait_ge(s["summed"], n[j])
                nc.vector.tensor_scalar(nq[:, j, 0], nq[:, j, 0], 1.0 / GD, 1e-6, ALU.mult, ALU.add).then_inc(s["q_eps"], 1)
                for m, (a, b) in enumerate(((0, GH), (GH, HQK))):
                    c = b - a
                    nc.vector.tensor_tensor(ra[:, j, a:b], qs[:, j, a:b], rot[:, 2 * m].unsqueeze(1).to_broadcast([P, c, GD]), ALU.mult)
                    nc.vector.tensor_tensor(rb[:, a:b, 0:half], qs[:, j, a:b, half:], rot[:, 2 * m + 1, 0:half].unsqueeze(1).to_broadcast([P, c, half]), ALU.mult)
                    last = nc.vector.tensor_tensor(rb[:, a:b, half:], qs[:, j, a:b, 0:half], rot[:, 2 * m + 1, half:].unsqueeze(1).to_broadcast([P, c, half]), ALU.mult)
                last.then_inc(s["rope_b"], 1)
                dve.wait_ge(s["rope_b"], n[j])
                nc.vector.tensor_tensor(ra[:, j], ra[:, j], rb[:], ALU.add).then_inc(s["roped"], 1)

            def softmax(j, n, turn):
                S = BIG.rearrange("p b (c m) -> p b c m", c=4)
                dve.wait_ge(s["s_psum"], n[j])
                nc.vector.tensor_reduce(mx[:, j, 0].rearrange("p (b c) -> p b c", b=4), S, X, ALU.max).then_inc(s["row_max"], 1)
                dve.wait_ge(s["row_max"], n[j])
                for b in range(4):
                    last = nc.vector.tensor_tensor(pr[:, j, 4 * b:4 * b + 4], S[:, b], mx[:, j, 0, 4 * b:4 * b + 4].unsqueeze(2).to_broadcast([P, 4, P]), ALU.subtract)
                last.then_inc(s["shifted"], 1)

            def sums(j, n, turn):
                dve.wait_ge(s["exped"], n[j])
                nc.vector.tensor_reduce(mx[:, j, 1], pr[:, j], X, ALU.add).then_inc(s["row_sum"], 1)
                dve.wait_ge(s["row_sum"], n[j])
                nc.vector.reciprocal(mx[:, j, 2], mx[:, j, 1]).then_inc(s["row_recip"], 1)
                dve.wait_ge(s["row_recip"], n[j])
                nc.vector.tensor_tensor(pr[:, j], pr[:, j], mx[:, j, 2].unsqueeze(2).to_broadcast([P, GH, P]), ALU.mult).then_inc(s["p_norm"], 1)

            def residual(j, n, turn):
                dve.wait_ge(s["y_psum"], n[j])
                dve.wait_ge(s["kept"], n[j] + 2)
                dve.wait_ge(s[f"stored{j}"], turn * 16)
                nc.vector.tensor_tensor(y[:, j], M[:, j, 0:D], xr[:, j], ALU.add).then_inc(s["y"], 1)

            def body(front, back):
                if front is not None:
                    n, turn = tiles(dve, front), front + 1
                    for stage in (norm, rms, scale):
                        for j in range(PAIR):
                            stage(j, n, turn)
                if back is not None:
                    m, before = tiles(dve, back), back + 1
                    for stage in (softmax, sums):
                        for j in range(PAIR):
                            stage(j, m, before)
                if front is not None:
                    for j in range(PAIR):
                        rope(j, n, turn)
                if back is not None:
                    for j in range(PAIR):
                        residual(j, m, before)

            overlapped(dve, body)

        @block.tensor
        def _(pe):
            pe.wait_ge(s["mask_made"], 2)
            wk, wv, wq = (w(m).rearrange("p (c o) -> p c o", c=DC) for m in ("wk", "wv", "wq"))
            wo = w("wo").rearrange("p (c o) -> p c o", c=GH)
            def turn_h(j, n, t):
                pe.wait_ge(s["scaled"], n[j])
                for ic in range(DC):
                    last = nc.tensor.transpose(M[:, j, ic * P:(ic + 1) * P], h[:, j, ic * P:(ic + 1) * P], k["ident"][:])
                last.then_inc(s["hT_psum"], 1)

            def keys(j, n, t):
                pe.wait_ge(s["hT"], n[j])
                for ic in range(DC):
                    last = nc.tensor.matmul(M[:, j], hT[:, j, ic], wk[:, ic], start=ic == 0, stop=ic == DC - 1)
                last.then_inc(s["k_psum"], 1)

            def values(j, n, t):
                pe.wait_ge(s["k_copied"], n[j])
                for ic in range(DC):
                    last = nc.tensor.matmul(M[:, j], hT[:, j, ic], wv[:, ic], start=ic == 0, stop=ic == DC - 1)
                last.then_inc(s["v_psum"], 1)

            def queries(j, n, t, m):
                if m is None:
                    if j == 1:
                        pe.wait_ge(s["q_copied"], n[0])
                elif j == 0:
                    pe.wait_ge(s["shifted"], m[1])
                else:
                    pe.wait_ge(s["oT"], m[1] + 1)
                for b in range(4):
                    for ic in range(DC):
                        last = nc.tensor.matmul(BIG[:, b], hT[:, j, ic], wq[:, ic, b * 512:(b + 1) * 512], start=ic == 0, stop=ic == DC - 1)
                last.then_inc(s["q_psum"], 1)

            def turn(buf, j, t, groups, first):
                for g in range(groups):
                    pe.wait_ge(s["evacuated"], t * SEQ + (first + g + 1))
                    for c in range(4):
                        last = nc.tensor.transpose(TP[:, (first + g) % 2, c], buf[:, j, 4 * g + c], k["ident"][:])
                    last.then_inc(s["turned"], 1)

            def turn_qk(j, n, t):
                pe.wait_ge(s["qk_scaled"], n[j])
                turn(ra, j, t, HQK // 4, j * (HQK // 4))

            def scores(j, n, t):
                pe.wait_ge(s["evacuated"], t * SEQ + ((j + 1) * (HQK // 4) + 2))
                if j == 0:
                    pe.wait_ge(s["q_copied"], n[1])
                else:
                    pe.wait_ge(s["shifted"], n[0])
                for b in range(4):
                    nc.tensor.matmul(BIG[:, b], k["ident_b"][:], cmask[:].rearrange("p c m -> p (c m)"), start=True, stop=False, skip_group_check=True)
                    for c in range(4):
                        last = nc.tensor.matmul(BIG[:, b, c * P:(c + 1) * P], qkT[:, j, 4 * b + c], qkT[:, j, GH + b],
                                                start=False, stop=c == 3, skip_group_check=True)
                last.then_inc(s["s_psum"], 1)

            def turn_p(j, n, t):
                pe.wait_ge(s["p_norm"], n[j])
                turn(pr, j, t, GH // 4, PAIR * (HQK // 4) + j * (GH // 4))

            def attend(j, n, t, front):
                pe.wait_ge(s["evacuated"], t * SEQ + (PAIR * (HQK // 4) + (j + 1) * (GH // 4) + 2))
                if j == 1:
                    pe.wait_ge(s["oT"], n[0] + 1)
                elif front is not None:
                    pe.wait_ge(s["q_copied"], front[0])
                else:
                    pe.wait_ge(s["shifted"], n[1])
                for b in range(4):
                    last = nc.tensor.matmul(BIG[:, b], v[:, j, b], pT[:, j, 4 * b:4 * b + 4].rearrange("p c m -> p (c m)"), start=True, stop=True)
                last.then_inc(s["oT_psum"], 1)

            def project(j, n, t):
                pe.wait_ge(s["oT"], n[j] + 1)
                for c in range(GH):
                    last = nc.tensor.matmul(M[:, j, 0:D], pr[:, j, c], wo[:, c], start=c == 0, stop=c == GH - 1)
                last.then_inc(s["y_psum"], 1)

            def body(front, back):
                n = tiles(pe, front) if front is not None else None
                m = tiles(pe, back) if back is not None else None

                def run(stages, count, t):
                    if t is not None:
                        for stage in stages:
                            for j in range(PAIR):
                                stage(j, count, t)

                if back is not None:
                    turn_qk(0, m, back)
                    scores(0, m, back)
                    if front is not None:
                        pe.wait_ge(s["y"], m[0])
                run((turn_h, keys), n, front)
                if back is not None:
                    turn_qk(1, m, back)
                    scores(1, m, back)
                run((values,), n, front)
                if front is not None:
                    queries(0, n, front, m)
                run((turn_p,), m, back)
                if back is not None:
                    for j in range(PAIR):
                        attend(j, m, back, n)
                if front is not None:
                    queries(1, n, front, m)
                if back is not None:
                    for j in range(PAIR):
                        pe.wait_ge(s["v_copied"], (n or m)[j])
                        project(j, m, back)

            overlapped(pe, body)
    end_phase(nc, s)


def moe(nc, k, layout, x_in, src_in, out, arena, load_next):
    first = "norm" in layout
    G = EI if first else GU3
    SETS = E if first else E + 2
    DN = -(-G // P)
    CH = [(c, min(512, G - c)) for c in range(0, G, 512)]
    TG = -(-DN // 4)
    SEQ = PAIR * len(CH)
    with ExitStack() as ctx:
        def sb(name, shape, dt=F32):
            return ctx.enter_context(nc.sbuf_tensor(("moe0_" if first else "moe3_") + name, shape, dt))

        def w(name):
            return part(arena, layout, name)

        s = semaphores(nc, ctx, ("moe0_" if first else "moe3_"), """
            tables ones weights_next x_loaded0 x_loaded1 h_loaded0 h_loaded1 stored0 stored1 biased srcT_psum srcT p_psum summed
            stats mean square var rstd tok res tokT_psum tokT logit_psum lmax shifted exped esum erecip prob top gt eq top2 pick thr sel
            comb wsum wrecip weights g_psum u_psum silu h_part h_done turned evacuated y_psum y""")
        GB = k["psum"][:, 0:2, :]
        UB = k["psum"][:, 2:4, :]
        TP = k["psum"][:, 4:6, :].rearrange("p r (c m) -> p r c m", c=4)
        M = k["psum"][:, 6:8, :]
        index = sb("index", [P, 2, E])
        xt = sb("xt", [P, PAIR, D])
        ht = sb("ht", [P, PAIR, D])
        st = sb("st", [P, PAIR, 6])
        mv = sb("mv", [P, PAIR, 2])
        sm = sb("sm", [P, PAIR, 12])
        srcT = sb("srcT", [P, PAIR, DC, P])
        tok = sb("tok", [P, PAIR, D])
        tokT = sb("tokT", [P, PAIR, DC, P])
        rt = sb("rt", [P, PAIR, 10, E])
        cw = sb("cw", [P, PAIR, SETS])
        sg = sb("sg", [P, 2, 512])
        h = sb("h", [P, PAIR, G])
        hT = sb("hT", [P, PAIR, 4 * TG, P])
        y = sb("y", [P, PAIR, D])
        block = ctx.enter_context(nc.Block())

        @block.sync
        def _(sp):
            with sp.Fori(0, NI) as i:
                for j in range(PAIR):
                    for sem in ("tok", "res") if first else ("srcT",):
                        sp.wait_ge(s[sem], i * PAIR + 1)
                    sp.dma_start(ht[:, j], src_in[i * PAIR + j]).then_inc(s[f"h_loaded{j}"], 16)
                for j in range(PAIR):
                    sp.wait_ge(s["y"], i * PAIR + 1)
                    sp.dma_start(xt[:, j], x_in[i * PAIR + j]).then_inc(s[f"x_loaded{j}"], 16)
            for step in load_next:
                step(sp, s["weights_next"])

        @block.gpsimd
        def _(pool):
            nc.gpsimd.iota(index[:, 0], pattern=[[-1, E]], base=E, channel_multiplier=0, allow_small_or_imprecise_dtypes=True)
            nc.gpsimd.iota(index[:, 1], pattern=[[1, E]], base=1, channel_multiplier=0, allow_small_or_imprecise_dtypes=True).then_inc(s["tables"], 1)
            with pool.Fori(0, NI) as i:
                n, turn = tiles(pool, i), pool.snap(i + 1)
                for j in range(PAIR):
                    if first:
                        pool.wait_ge(s[f"x_loaded{j}"], turn * 16)
                        pool.wait_ge(s[f"h_loaded{j}"], turn * 16)
                        nc.gpsimd.tensor_tensor(xt[:, j], xt[:, j], ht[:, j], ALU.add).then_inc(s["res"], 1)
                    else:
                        pool.wait_ge(s[f"x_loaded{j}"], turn * 16)
                        nc.gpsimd.tensor_tensor(xt[:, j], xt[:, j], w("bp"), ALU.add).then_inc(s["biased"], 1)
                for j in range(PAIR):
                    pool.wait_ge(s["var"], n[j])
                    nc.gpsimd.tensor_tensor(sm[:, j, 1:2], sm[:, j, 0:1], k["neg_half"][:], ALU.pow).then_inc(s["rstd"], 1)
                for j in range(PAIR):
                    pool.wait_ge(s["weights"], n[j])
                    pool.wait_ge(s["h_part"], i * SEQ + ((j + 1) * len(CH) + 2))
                    nc.gpsimd.tensor_tensor(h[:, j].rearrange("p (e i) -> p e i", i=I), h[:, j].rearrange("p (e i) -> p e i", i=I),
                                            cw[:, j].unsqueeze(2).to_broadcast([P, SETS, I]), ALU.mult).then_inc(s["h_done"], 1)

        @block.scalar
        def _(act):
            with act.Fori(0, NI) as i:
                n = tiles(act, i)

                def turned_src(j):
                    act.wait_ge(s["srcT_psum"], n[j])
                    nc.scalar.copy(srcT[:, j], M[:, j, 0:DC * P]).then_inc(s["srcT"], 1)

                def turned_tok(j):
                    act.wait_ge(s["tokT_psum"], n[j])
                    nc.scalar.copy(tokT[:, j], M[:, j, 0:DC * P]).then_inc(s["tokT"], 1)

                def exp(j):
                    act.wait_ge(s["shifted"], n[j])
                    nc.scalar.activation(rt[:, j, 1], rt[:, j, 0], ACT.Exp).then_inc(s["exped"], 1)

                def silu(j):
                    for c, (at, size) in enumerate(CH):
                        q = j * len(CH) + c
                        act.wait_ge(s["g_psum"], i * SEQ + (q + 1))
                        act.wait_ge(s["h_part"], i * SEQ + (q + 1))
                        nc.scalar.activation(sg[:, q % 2, 0:size], GB[:, q % 2, 0:size], ACT.Silu).then_inc(s["silu"], 1)

                def turned_h(j):
                    for g in range(TG):
                        q = j * TG + g
                        act.wait_ge(s["turned"], i * (PAIR * TG) + (q + 1))
                        full = min(4 * g + 4, G // P) - 4 * g
                        last = nc.scalar.copy(hT[:, j, 4 * g:4 * g + full], TP[:, q % 2, 0:full])
                        if g == TG - 1 and G % P:
                            last = nc.scalar.copy(hT[0:G % P, j, G // P], TP[0:G % P, q % 2, full])
                        last.then_inc(s["evacuated"], 1)

                def store(j):
                    act.wait_ge(s["y"], n[j] + 1)
                    act.dma_start(out[i * PAIR + j], y[:, j]).then_inc(s[f"stored{j}"], 16)

                for stage in (() if first else (turned_src,)) + (turned_tok, exp, silu, turned_h, store):
                    for j in range(PAIR):
                        stage(j)
            for j in range(PAIR):
                act.wait_ge(s[f"stored{j}"], (NI + 1) * 16)

        @block.vector
        def _(dve):
            credit(nc, k, s, y=1, h_part=2, evacuated=2, stored0=16, stored1=16, **(dict(tok=1, res=1) if first else dict(srcT=1)))
            if not first:
                nc.vector.memset(cw[:], 1.0).then_inc(s["ones"], 1)
                dve.wait_ge(s["ones"], 1)
            dve.wait_ge(s["tables"], 1)
            src = ht if first else xt

            def project(j, n, turn):
                dve.wait_ge(s["p_psum"], n[j])
                dve.wait_ge(s["biased"], n[j])
                nc.vector.tensor_tensor(xt[:, j], M[:, j, 0:D], xt[:, j], ALU.add).then_inc(s["summed"], 1)

            def stats(j, n, turn):
                if first:
                    dve.wait_ge(s[f"h_loaded{j}"], turn * 16)
                else:
                    dve.wait_ge(s["summed"], n[j])
                nc.vector.bn_stats(st[:, j], src[:, j]).then_inc(s["stats"], 1)
                hold(dve, k["scratch"][:, j:j + 1], s["stats"], n[j])
                nc.vector.bn_aggr(mv[:, j], st[:, j]).then_inc(s["mean"], 1)
                dve.wait_ge(s["mean"], n[j])
                if first:
                    nc.vector.scalar_tensor_tensor(sm[:, j, 2:3], mv[:, j, 0:1], mv[:, j, 0:1], mv[:, j, 1:2], ALU.mult, ALU.add).then_inc(s["square"], 1)
                    dve.wait_ge(s["square"], n[j])
                    nc.vector.tensor_scalar(sm[:, j, 0:1], sm[:, j, 2:3], 1e-6, None, ALU.add).then_inc(s["var"], 1)
                else:
                    nc.vector.tensor_scalar(sm[:, j, 0:1], mv[:, j, 1:2], 1e-5, None, ALU.add).then_inc(s["var"], 1)

            def norm(j, n, turn):
                dve.wait_ge(s["rstd"], n[j])
                if first:
                    nc.vector.scalar_tensor_tensor(tok[:, j], ht[:, j], sm[:, j, 1:2], w("norm"), ALU.mult, ALU.mult).then_inc(s["tok"], 1)
                else:
                    nc.vector.tensor_scalar(tok[:, j], xt[:, j], mv[:, j, 0:1], sm[:, j, 1:2], ALU.subtract, ALU.mult).then_inc(s["tok"], 1)

            def logits(j, n, turn):
                L = M[:, j, D:D + E]
                dve.wait_ge(s["logit_psum"], n[j])
                nc.vector.tensor_reduce(sm[:, j, 3:4], L, X, ALU.max).then_inc(s["lmax"], 1)
                dve.wait_ge(s["lmax"], n[j])
                nc.vector.tensor_scalar(rt[:, j, 0], L, sm[:, j, 3:4], None, ALU.subtract).then_inc(s["shifted"], 1)

            def route(j, n, turn):
                prob, best, above, tied, best2, pick, sel = (rt[:, j, m] for m in range(2, 9))
                dve.wait_ge(s["exped"], n[j])
                nc.vector.tensor_reduce(sm[:, j, 4:5], rt[:, j, 1], X, ALU.add).then_inc(s["esum"], 1)
                dve.wait_ge(s["esum"], n[j])
                nc.vector.reciprocal(sm[:, j, 5:6], sm[:, j, 4:5]).then_inc(s["erecip"], 1)
                dve.wait_ge(s["erecip"], n[j])
                nc.vector.tensor_scalar(prob, rt[:, j, 1], sm[:, j, 5:6], None, ALU.mult).then_inc(s["prob"], 1)
                hold(dve, k["scratch"][:, 2 + j:3 + j], s["prob"], n[j])
                nc.vector.max(best, prob).then_inc(s["top"], 1)
                dve.wait_ge(s["top"], n[j])
                nc.vector.tensor_scalar(above, prob, best[:, 1:2], 0.0, ALU.is_gt, ALU.add, accum_out=sm[:, j, 6:7]).then_inc(s["gt"], 1)
                nc.vector.scalar_tensor_tensor(tied, prob, best[:, 1:2], index[:, 0], ALU.is_equal, ALU.mult).then_inc(s["eq"], 1)
                hold(dve, k["scratch"][:, 4 + j:5 + j], s["eq"], n[j])
                nc.vector.max(best2, tied).then_inc(s["top2"], 1)
                dve.wait_ge(s["gt"], n[j])
                nc.vector.tensor_scalar(pick, index[:, 1], sm[:, j, 6:7], 2.0, ALU.add, ALU.is_equal).then_inc(s["pick"], 1)
                dve.wait_ge(s["pick"], n[j])
                dve.wait_ge(s["top2"], n[j])
                nc.vector.tensor_tensor_reduce(pick, pick, best2, 1.0, 0.0, ALU.mult, ALU.add, sm[:, j, 7:8]).then_inc(s["thr"], 1)
                dve.wait_ge(s["thr"], n[j])
                nc.vector.scalar_tensor_tensor(sel, tied, sm[:, j, 7:8], above, ALU.is_ge, ALU.add).then_inc(s["sel"], 1)
                dve.wait_ge(s["sel"], n[j])
                nc.vector.tensor_tensor_reduce(rt[:, j, 9], prob, sel, 1.0, 0.0, ALU.mult, ALU.add, sm[:, j, 8:9]).then_inc(s["comb"], 1)
                dve.wait_ge(s["comb"], n[j])
                nc.vector.tensor_scalar(sm[:, j, 9:10], sm[:, j, 8:9], 1e-9 if first else 1e-20, None, ALU.add).then_inc(s["wsum"], 1)
                dve.wait_ge(s["wsum"], n[j])
                nc.vector.reciprocal(sm[:, j, 10:11], sm[:, j, 9:10]).then_inc(s["wrecip"], 1)
                dve.wait_ge(s["wrecip"], n[j])
                nc.vector.tensor_scalar(cw[:, j, 0:E], rt[:, j, 9], sm[:, j, 10:11], None, ALU.mult).then_inc(s["weights"], 1)

            def products(i, j, n):
                for c, (at, size) in enumerate(CH):
                    q = j * len(CH) + c
                    dve.wait_ge(s["silu"], i * SEQ + (q + 1))
                    dve.wait_ge(s["u_psum"], i * SEQ + (q + 1))
                    nc.vector.tensor_tensor(h[:, j, at:at + size], sg[:, q % 2, 0:size], UB[:, q % 2, 0:size], ALU.mult).then_inc(s["h_part"], 1)

            def residual(j, n, turn):
                dve.wait_ge(s["y_psum"], n[j])
                if first:
                    dve.wait_ge(s["res"], n[j] + 1)
                dve.wait_ge(s[f"stored{j}"], turn * 16)
                nc.vector.tensor_tensor(y[:, j], M[:, j, 0:D], xt[:, j], ALU.add).then_inc(s["y"], 1)

            with dve.Fori(0, NI) as i:
                n, turn = tiles(dve, i), dve.snap(i + 1)
                for stage in (() if first else (project,)) + (stats, norm, logits, route):
                    for j in range(PAIR):
                        stage(j, n, turn)
                for j in range(PAIR):
                    products(i, j, n)
                for j in range(PAIR):
                    residual(j, n, turn)

        @block.tensor
        def _(pe):
            pe.wait_ge(s["tables"], 1)
            wg, wu, gate = (w(m).rearrange("p (c o) -> p c o", c=DC) for m in ("wg", "wu", "gate"))
            wd = w("wd").rearrange("p (c o) -> p c o", c=DN)
            with pe.Fori(0, NI) as i:
                n, turn = tiles(pe, i), pe.snap(i + 1)

                def turn_src(j):
                    pe.wait_ge(s[f"h_loaded{j}"], turn * 16)
                    for ic in range(DC):
                        last = nc.tensor.transpose(M[:, j, ic * P:(ic + 1) * P], ht[:, j, ic * P:(ic + 1) * P], k["ident"][:])
                    last.then_inc(s["srcT_psum"], 1)

                def project(j):
                    wp = w("wp").rearrange("p (c o) -> p c o", c=DC)
                    pe.wait_ge(s["srcT"], n[j] + 1)
                    for ic in range(DC):
                        last = nc.tensor.matmul(M[:, j, 0:D], srcT[:, j, ic], wp[:, ic], start=ic == 0, stop=ic == DC - 1)
                    last.then_inc(s["p_psum"], 1)

                def turn_tok(j):
                    pe.wait_ge(s["tok"], n[j] + 1 if first else n[j])
                    for ic in range(DC):
                        last = nc.tensor.transpose(M[:, j, ic * P:(ic + 1) * P], tok[:, j, ic * P:(ic + 1) * P], k["ident"][:])
                    last.then_inc(s["tokT_psum"], 1)

                def logits(j):
                    pe.wait_ge(s["tokT"], n[j])
                    for ic in range(DC):
                        last = nc.tensor.matmul(M[:, j, D:D + E], tokT[:, j, ic], gate[:, ic], start=ic == 0, stop=ic == DC - 1)
                    last.then_inc(s["logit_psum"], 1)

                def gate_up(j):
                    for c, (at, size) in enumerate(CH):
                        q = j * len(CH) + c
                        pe.wait_ge(s["h_part"], i * SEQ + (q + 1))
                        for bank, wt, sem in ((GB, wg, "g_psum"), (UB, wu, "u_psum")):
                            for ic in range(DC):
                                last = nc.tensor.matmul(bank[:, q % 2, 0:size], tokT[:, j, ic], wt[:, ic, at:at + size], start=ic == 0, stop=ic == DC - 1)
                            last.then_inc(s[sem], 1)

                def turn_h(j):
                    pe.wait_ge(s["h_done"], n[j])
                    for g in range(TG):
                        q = j * TG + g
                        pe.wait_ge(s["evacuated"], i * (PAIR * TG) + (q + 1))
                        for c in range(4 * g, min(4 * g + 4, DN)):
                            size = min(P, G - c * P)
                            last = nc.tensor.transpose(TP[0:size, q % 2, c % 4], h[:, j, c * P:c * P + size], k["ident"][:])
                        last.then_inc(s["turned"], 1)

                def down(j):
                    pe.wait_ge(s["evacuated"], i * (PAIR * TG) + ((j + 1) * TG + 2))
                    for c in range(DN):
                        size = min(P, G - c * P)
                        last = nc.tensor.matmul(M[:, j, 0:D], hT[0:size, j, c], wd[0:size, c], start=c == 0, stop=c == DN - 1)
                    last.then_inc(s["y_psum"], 1)

                pe.wait_ge(s["y"], i * PAIR + 1)
                for stage in (() if first else (turn_src, project)) + (turn_tok, logits, gate_up):
                    for j in range(PAIR):
                        stage(j)
                for j in range(PAIR):
                    turn_h(j)
                    down(j)
    end_phase(nc, s)


def xmask(nc, k, x_in, x_out, ctx_T, ctx_rows, masks, load_next):
    with ExitStack() as ctx:
        def sb(name, shape, dt=F32):
            return ctx.enter_context(nc.sbuf_tensor("xmask_" + name, shape, dt))

        s = semaphores(nc, ctx, "xmask_", """
            weights_next x_loaded0 x_loaded1 ct_loaded0 ct_loaded1 c_loaded0 c_loaded1 m_loaded0 m_loaded1 stored0 stored1
            mask_float stats mean var rstd normed neg_mask valid xT_psum xT s_psum kept masked row_max bias exped recip factor
            pT_psum pT y_psum y""")
        M = k["psum"][:, 6:8, :]
        xt = sb("xt", [P, PAIR, D])
        ct = sb("ct", [P, PAIR, DC, P])
        cr = sb("cr", [P, PAIR, D])
        mi = sb("mi", [P, PAIR, P], mybir.dt.int32)
        mf = sb("mf", [P, PAIR, P])
        nm = sb("nm", [P, PAIR, P])
        st = sb("st", [P, PAIR, 6])
        mv = sb("mv", [P, PAIR, 2])
        sm = sb("sm", [P, PAIR, 8])
        xn = sb("xn", [P, PAIR, D])
        xT = sb("xT", [P, PAIR, DC, P])
        pr = sb("pr", [P, PAIR, P])
        pT = sb("pT", [P, PAIR, P])
        y = sb("y", [P, PAIR, D])
        block = ctx.enter_context(nc.Block())

        @block.sync
        def _(sp):
            with sp.Fori(0, NI) as i:
                for j in range(PAIR):
                    sp.wait_ge(s["y"], i * PAIR + 1)
                    for dst, src, sem in ((xt, x_in, "x"), (mi, masks, "m"), (ct, ctx_T, "ct"), (cr, ctx_rows, "c")):
                        sp.dma_start(dst[:, j], src[i * PAIR + j]).then_inc(s[f"{sem}_loaded{j}"], 16)
            for step in load_next:
                step(sp, s["weights_next"])

        @block.gpsimd
        def _(pool):
            with pool.Fori(0, NI) as i:
                n = tiles(pool, i)
                for j in range(PAIR):
                    pool.wait_ge(s["var"], n[j])
                    nc.gpsimd.tensor_tensor(sm[:, j, 1:2], sm[:, j, 0:1], k["neg_half"][:], ALU.pow).then_inc(s["rstd"], 1)

        @block.scalar
        def _(act):
            with act.Fori(0, NI) as i:
                n, turn = tiles(act, i), act.snap(i + 1)

                def mask(j):
                    act.wait_ge(s[f"m_loaded{j}"], turn * 16)
                    nc.scalar.copy(mf[:, j], mi[:, j]).then_inc(s["mask_float"], 1)

                def turned_x(j):
                    act.wait_ge(s["xT_psum"], n[j])
                    nc.scalar.copy(xT[:, j], M[:, j, 0:DC * P]).then_inc(s["xT"], 1)

                def exp(j):
                    act.wait_ge(s["bias"], n[j])
                    nc.scalar.activation(pr[:, j], pr[:, j], ACT.Exp, bias=sm[:, j, 3:4], scale=D ** -0.5,
                                         accum_out=sm[:, j, 4:5]).then_inc(s["exped"], 1)

                def turned_p(j):
                    act.wait_ge(s["pT_psum"], n[j])
                    nc.scalar.copy(pT[:, j], M[:, j, P:2 * P]).then_inc(s["pT"], 1)

                def store(j):
                    act.wait_ge(s["y"], n[j] + 1)
                    act.dma_start(x_out[i * PAIR + j], y[:, j]).then_inc(s[f"stored{j}"], 16)

                for stage in (mask, turned_x, exp, turned_p, store):
                    for j in range(PAIR):
                        stage(j)
            for j in range(PAIR):
                act.wait_ge(s[f"stored{j}"], (NI + 1) * 16)

        @block.vector
        def _(dve):
            credit(nc, k, s, y=1, stored0=16, stored1=16)

            def norm(j, n, turn):
                dve.wait_ge(s[f"x_loaded{j}"], turn * 16)
                nc.vector.bn_stats(st[:, j], xt[:, j]).then_inc(s["stats"], 1)
                hold(dve, k["scratch"][:, j:j + 1], s["stats"], n[j])
                nc.vector.bn_aggr(mv[:, j], st[:, j]).then_inc(s["mean"], 1)
                dve.wait_ge(s["mean"], n[j])
                nc.vector.tensor_scalar(sm[:, j, 0:1], mv[:, j, 1:2], 1e-5, None, ALU.add).then_inc(s["var"], 1)

            def mask(j, n, turn):
                dve.wait_ge(s["mask_float"], n[j])
                nc.vector.tensor_scalar(nm[:, j], mf[:, j], 1.0, -NEG, ALU.subtract, ALU.mult).then_inc(s["neg_mask"], 1)
                nc.vector.tensor_reduce(sm[:, j, 5:6], mf[:, j], X, ALU.max).then_inc(s["valid"], 1)

            def scaled(j, n, turn):
                dve.wait_ge(s["rstd"], n[j])
                nc.vector.tensor_scalar(xn[:, j], xt[:, j], mv[:, j, 0:1], sm[:, j, 1:2], ALU.subtract, ALU.mult).then_inc(s["normed"], 1)

            def softmax(j, n, turn):
                dve.wait_ge(s["s_psum"], n[j])
                nc.vector.tensor_tensor(pr[:, j], M[:, j, 0:P], mf[:, j], ALU.mult).then_inc(s["kept"], 1)
                dve.wait_ge(s["kept"], n[j])
                dve.wait_ge(s["neg_mask"], n[j])
                nc.vector.tensor_tensor(pr[:, j], pr[:, j], nm[:, j], ALU.add).then_inc(s["masked"], 1)
                dve.wait_ge(s["masked"], n[j])
                nc.vector.tensor_reduce(sm[:, j, 2:3], pr[:, j], X, ALU.max).then_inc(s["row_max"], 1)
                dve.wait_ge(s["row_max"], n[j])
                nc.vector.tensor_scalar(sm[:, j, 3:4], sm[:, j, 2:3], -(D ** -0.5), None, ALU.mult).then_inc(s["bias"], 1)

            def factor(j, n, turn):
                dve.wait_ge(s["exped"], n[j])
                nc.vector.reciprocal(sm[:, j, 6:7], sm[:, j, 4:5]).then_inc(s["recip"], 1)
                dve.wait_ge(s["recip"], n[j])
                dve.wait_ge(s["valid"], n[j])
                nc.vector.tensor_tensor(sm[:, j, 7:8], sm[:, j, 6:7], sm[:, j, 5:6], ALU.mult).then_inc(s["factor"], 1)

            def residual(j, n, turn):
                dve.wait_ge(s["factor"], n[j])
                dve.wait_ge(s["y_psum"], n[j])
                dve.wait_ge(s[f"stored{j}"], turn * 16)
                nc.vector.scalar_tensor_tensor(y[:, j], M[:, j, D:2 * D], sm[:, j, 7:8], xt[:, j], ALU.mult, ALU.add).then_inc(s["y"], 1)

            with dve.Fori(0, NI) as i:
                n, turn = tiles(dve, i), dve.snap(i + 1)
                for stage in (norm, mask, scaled, softmax, factor, residual):
                    for j in range(PAIR):
                        stage(j, n, turn)

        @block.tensor
        def _(pe):
            with pe.Fori(0, NI) as i:
                n, turn = tiles(pe, i), pe.snap(i + 1)

                def turn_x(j):
                    pe.wait_ge(s["normed"], n[j])
                    for ic in range(DC):
                        last = nc.tensor.transpose(M[:, j, ic * P:(ic + 1) * P], xn[:, j, ic * P:(ic + 1) * P], k["ident"][:])
                    last.then_inc(s["xT_psum"], 1)

                def scores(j):
                    pe.wait_ge(s[f"ct_loaded{j}"], turn * 16)
                    pe.wait_ge(s["xT"], n[j])
                    for ic in range(DC):
                        last = nc.tensor.matmul(M[:, j, 0:P], xT[:, j, ic], ct[:, j, ic], start=ic == 0, stop=ic == DC - 1)
                    last.then_inc(s["s_psum"], 1)

                def turn_p(j):
                    pe.wait_ge(s["exped"], n[j])
                    nc.tensor.transpose(M[:, j, P:2 * P], pr[:, j], k["ident"][:]).then_inc(s["pT_psum"], 1)

                def attend(j):
                    pe.wait_ge(s[f"c_loaded{j}"], turn * 16)
                    pe.wait_ge(s["pT"], n[j])
                    nc.tensor.matmul(M[:, j, D:2 * D], pT[:, j], cr[:, j], start=True, stop=True).then_inc(s["y_psum"], 1)

                pe.wait_ge(s["y"], i * PAIR + 1)
                for stage in (turn_x, scores, turn_p, attend):
                    for j in range(PAIR):
                        stage(j)
    end_phase(nc, s)


def bit(nc, k, x_in, x_out, arena, load_next):
    FC = F // P
    HALF = F // 2
    CH = 2
    SEQ = PAIR * CH
    with ExitStack() as ctx:
        def sb(name, shape, dt=F32):
            return ctx.enter_context(nc.sbuf_tensor("bit_" + name, shape, dt))

        def w(name):
            return part(arena, W_BIT, name)

        s = semaphores(nc, ctx, "bit_", """
            weights_next w_sums w_total w_mean w_recip w_round w_low w_ternary c1 c2
            x_loaded0 x_loaded1 stored0 stored1 stats mean var rstd normed amax clipped recip recip127 rounded quantised
            xT_psum xT s1 s2 s3 cf g_psum u_psum relu square act_part act_g squares amax2
            m1 m2 m3 var2 rstd2 kf ay clip2 r2 k2 k3 rounded2 quantised2 hT_psum hT out1 out2 y_psum y""")
        GB = k["psum"][:, 0:2, :]
        UB = k["psum"][:, 2:4, :]
        M = k["psum"][:, 6:8, :]
        MB = M.rearrange("p j c -> p (j c)").bitcast(BF16).rearrange("p (j c) -> p j c", j=PAIR)
        TP = k["psum"][:, 4:6, :].rearrange("p j c -> p (j c)").bitcast(BF16).rearrange("p (j c m) -> p j c m", j=PAIR, m=P)
        ws = sb("ws", [P, 6, 3])
        wt = sb("wt", [P, DC * F])
        wb = sb("wb", [P, 3, DC * F], BF16)
        xt = sb("xt", [P, PAIR, D])
        st = sb("st", [P, PAIR, 6])
        mv = sb("mv", [P, PAIR, 2])
        sm = sb("sm", [P, PAIR, 24])
        xn = sb("xn", [P, PAIR, D])
        xq = sb("xq", [P, PAIR, D], BF16)
        xT = sb("xT", [P, PAIR, DC, P], BF16)
        rl = sb("rl", [P, 2, HALF])
        a = sb("a", [P, PAIR, F])
        ag = sb("ag", [P, PAIR, F])
        hq = sb("hq", [P, PAIR, F], BF16)
        hT = sb("hT", [P, PAIR, FC, P], BF16)
        y = sb("y", [P, PAIR, D])
        block = ctx.enter_context(nc.Block())

        @block.sync
        def _(sp):
            with sp.Fori(0, NI) as i:
                for j in range(PAIR):
                    sp.wait_ge(s["y"], i * PAIR + 1)
                    sp.dma_start(xt[:, j], x_in[i * PAIR + j]).then_inc(s[f"x_loaded{j}"], 16)
            for step in load_next:
                step(sp, s["weights_next"])

        @block.gpsimd
        def _(pool):
            pool.wait_ge(s["w_sums"], 3)
            nc.gpsimd.partition_all_reduce(ws[:, 1], ws[:, 0], P, RADD).then_inc(s["w_total"], 1)
            with pool.Fori(0, NI) as i:
                n = tiles(pool, i)
                for j in range(PAIR):
                    pool.wait_ge(s["var"], n[j])
                    nc.gpsimd.tensor_tensor(sm[:, j, 1:2], sm[:, j, 0:1], k["neg_half"][:], ALU.pow).then_inc(s["rstd"], 1)
                for j in range(PAIR):
                    pool.wait_ge(s["act_part"], i * SEQ + ((j + 1) * CH + 2))
                    nc.gpsimd.tensor_tensor(ag[:, j], a[:, j], w("g"), ALU.mult).then_inc(s["act_g"], 1)
                for j in range(PAIR):
                    pool.wait_ge(s["var2"], n[j])
                    nc.gpsimd.tensor_tensor(sm[:, j, 12:13], sm[:, j, 11:12], k["neg_half"][:], ALU.pow).then_inc(s["rstd2"], 1)

        @block.scalar
        def _(act):
            with act.Fori(0, NI) as i:
                n = tiles(act, i)

                def turned_x(j):
                    act.wait_ge(s["xT_psum"], n[j])
                    nc.scalar.copy(xT[:, j], MB[:, j, 0:DC * P]).then_inc(s["xT"], 1)

                def squared_relu(j):
                    for c in range(CH):
                        q = j * CH + c
                        act.wait_ge(s["g_psum"], i * SEQ + (q + 1))
                        act.wait_ge(s["act_part"], i * SEQ + (q + 1))
                        nc.scalar.activation(rl[:, q % 2], GB[:, q % 2], ACT.Relu).then_inc(s["relu"], 1)
                        act.wait_ge(s["relu"], i * SEQ + (q + 1))
                        nc.scalar.activation(rl[:, q % 2], rl[:, q % 2], ACT.Square).then_inc(s["square"], 1)

                def squares(j):
                    act.wait_ge(s["act_g"], n[j])
                    nc.scalar.activation(a[:, j], a[:, j], ACT.Square, accum_out=sm[:, j, 8:9]).then_inc(s["squares"], 1)

                def turned_h(j):
                    act.wait_ge(s["hT_psum"], n[j])
                    nc.scalar.copy(hT[:, j], TP[:, j]).then_inc(s["hT"], 1)

                def store(j):
                    act.wait_ge(s["y"], n[j] + 1)
                    act.dma_start(x_out[i * PAIR + j], y[:, j]).then_inc(s[f"stored{j}"], 16)

                for stage in (turned_x, squared_relu, squares, turned_h, store):
                    for j in range(PAIR):
                        stage(j)
            for j in range(PAIR):
                act.wait_ge(s[f"stored{j}"], (NI + 1) * 16)

        @block.vector
        def _(dve):
            credit(nc, k, s, y=1, act_part=2, stored0=16, stored1=16)
            for m, name in enumerate(("wg", "wu", "wd")):
                nc.vector.tensor_reduce(ws[:, 0, m:m + 1], w(name), X, ALU.add, apply_absolute_value=True).then_inc(s["w_sums"], 1)
            dve.wait_ge(s["w_total"], 1)
            nc.vector.tensor_scalar(ws[:, 2], ws[:, 1], 1.0 / (D * F), 1e-5, ALU.mult, ALU.max).then_inc(s["w_mean"], 1)
            dve.wait_ge(s["w_mean"], 1)
            nc.vector.reciprocal(ws[:, 3], ws[:, 2]).then_inc(s["w_recip"], 1)
            dve.wait_ge(s["w_recip"], 1)
            for m, name in enumerate(("wg", "wu", "wd")):
                if m:
                    dve.wait_ge(s["w_ternary"], m)
                nc.vector.tensor_scalar(wt[:], w(name), ws[:, 3, m:m + 1], MAGIC, ALU.mult, ALU.add).then_inc(s["w_round"], 1)
                dve.wait_ge(s["w_round"], m + 1)
                nc.vector.tensor_scalar(wt[:], wt[:], MAGIC, 1.0, ALU.subtract, ALU.min).then_inc(s["w_low"], 1)
                dve.wait_ge(s["w_low"], m + 1)
                nc.vector.tensor_scalar(wb[:, m], wt[:], -1.0, None, ALU.max).then_inc(s["w_ternary"], 1)
            nc.vector.tensor_tensor(ws[:, 4, 0:1], ws[:, 2, 0:1], ws[:, 2, 0:1], ALU.mult).then_inc(s["c1"], 1)
            dve.wait_ge(s["c1"], 1)
            nc.vector.tensor_tensor(ws[:, 4, 1:2], ws[:, 4, 0:1], ws[:, 2, 1:2], ALU.mult).then_inc(s["c2"], 1)
            dve.wait_ge(s["c2"], 1)

            def norm(j, n, turn):
                dve.wait_ge(s[f"x_loaded{j}"], turn * 16)
                nc.vector.bn_stats(st[:, j], xt[:, j]).then_inc(s["stats"], 1)
                hold(dve, k["scratch"][:, j:j + 1], s["stats"], n[j])
                nc.vector.bn_aggr(mv[:, j], st[:, j]).then_inc(s["mean"], 1)
                dve.wait_ge(s["mean"], n[j])
                nc.vector.tensor_scalar(sm[:, j, 0:1], mv[:, j, 1:2], 1e-5, None, ALU.add).then_inc(s["var"], 1)

            def quantise(j, n, turn):
                dve.wait_ge(s["rstd"], n[j])
                nc.vector.tensor_scalar(xn[:, j], xt[:, j], mv[:, j, 0:1], sm[:, j, 1:2], ALU.subtract, ALU.mult).then_inc(s["normed"], 1)
                dve.wait_ge(s["normed"], n[j])
                nc.vector.tensor_reduce(sm[:, j, 2:3], xn[:, j], X, ALU.max, apply_absolute_value=True).then_inc(s["amax"], 1)
                dve.wait_ge(s["amax"], n[j])
                nc.vector.tensor_scalar(sm[:, j, 3:4], sm[:, j, 2:3], 1e-5, 1.0 / 127.0, ALU.max, ALU.mult).then_inc(s["clipped"], 1)
                dve.wait_ge(s["clipped"], n[j])
                nc.vector.reciprocal(sm[:, j, 4:5], sm[:, j, 3:4]).then_inc(s["recip"], 1)
                dve.wait_ge(s["recip"], n[j])
                nc.vector.tensor_scalar(xn[:, j], xn[:, j], sm[:, j, 4:5], MAGIC, ALU.mult, ALU.add).then_inc(s["rounded"], 1)
                dve.wait_ge(s["rounded"], n[j])
                nc.vector.tensor_scalar(xq[:, j], xn[:, j], MAGIC, None, ALU.subtract).then_inc(s["quantised"], 1)
                nc.vector.tensor_tensor(sm[:, j, 5:6], sm[:, j, 3:4], sm[:, j, 3:4], ALU.mult).then_inc(s["s1"], 1)
                dve.wait_ge(s["s1"], n[j])
                nc.vector.tensor_tensor(sm[:, j, 6:7], sm[:, j, 5:6], sm[:, j, 3:4], ALU.mult).then_inc(s["s2"], 1)
                dve.wait_ge(s["s2"], n[j])
                nc.vector.tensor_tensor(sm[:, j, 7:8], sm[:, j, 6:7], ws[:, 4, 1:2], ALU.mult).then_inc(s["cf"], 1)

            def products(i, j):
                for c in range(CH):
                    q = j * CH + c
                    dve.wait_ge(s["u_psum"], i * SEQ + (q + 1))
                    dve.wait_ge(s["square"], i * SEQ + (q + 1))
                    nc.vector.tensor_tensor(a[:, j, c * HALF:(c + 1) * HALF], rl[:, q % 2], UB[:, q % 2], ALU.mult).then_inc(s["act_part"], 1)

            def subln(j, n, turn):
                dve.wait_ge(s["act_g"], n[j])
                nc.vector.tensor_reduce(sm[:, j, 13:14], ag[:, j], X, ALU.max, apply_absolute_value=True).then_inc(s["amax2"], 1)
                dve.wait_ge(s["squares"], n[j])
                dve.wait_ge(s["cf"], n[j])
                nc.vector.tensor_tensor(sm[:, j, 9:10], sm[:, j, 8:9], sm[:, j, 7:8], ALU.mult).then_inc(s["m1"], 1)
                dve.wait_ge(s["m1"], n[j])
                nc.vector.tensor_tensor(sm[:, j, 10:11], sm[:, j, 9:10], sm[:, j, 7:8], ALU.mult).then_inc(s["m2"], 1)
                dve.wait_ge(s["m2"], n[j])
                nc.vector.tensor_scalar(sm[:, j, 11:12], sm[:, j, 10:11], 1.0 / F, 1e-6, ALU.mult, ALU.add).then_inc(s["var2"], 1)

            def quantise2(j, n, turn):
                dve.wait_ge(s["rstd2"], n[j])
                nc.vector.tensor_tensor(sm[:, j, 14:15], sm[:, j, 12:13], sm[:, j, 7:8], ALU.mult).then_inc(s["kf"], 1)
                dve.wait_ge(s["kf"], n[j])
                dve.wait_ge(s["amax2"], n[j])
                nc.vector.tensor_tensor(sm[:, j, 15:16], sm[:, j, 13:14], sm[:, j, 14:15], ALU.mult).then_inc(s["ay"], 1)
                dve.wait_ge(s["ay"], n[j])
                nc.vector.tensor_scalar(sm[:, j, 16:17], sm[:, j, 15:16], 1e-5, 1.0 / 127.0, ALU.max, ALU.mult).then_inc(s["clip2"], 1)
                dve.wait_ge(s["clip2"], n[j])
                nc.vector.reciprocal(sm[:, j, 17:18], sm[:, j, 16:17]).then_inc(s["r2"], 1)
                nc.vector.tensor_tensor(sm[:, j, 19:20], sm[:, j, 16:17], ws[:, 2, 2:3], ALU.mult).then_inc(s["out1"], 1)
                dve.wait_ge(s["r2"], n[j])
                nc.vector.tensor_tensor(sm[:, j, 18:19], sm[:, j, 17:18], sm[:, j, 14:15], ALU.mult).then_inc(s["k2"], 1)
                dve.wait_ge(s["k2"], n[j])
                nc.vector.tensor_scalar(ag[:, j], ag[:, j], sm[:, j, 18:19], MAGIC, ALU.mult, ALU.add).then_inc(s["rounded2"], 1)
                dve.wait_ge(s["rounded2"], n[j])
                nc.vector.tensor_scalar(hq[:, j], ag[:, j], MAGIC, None, ALU.subtract).then_inc(s["quantised2"], 1)

            def residual(j, n, turn):
                dve.wait_ge(s["out1"], n[j])
                dve.wait_ge(s["y_psum"], n[j])
                dve.wait_ge(s[f"stored{j}"], turn * 16)
                nc.vector.scalar_tensor_tensor(y[:, j], M[:, j, 0:D], sm[:, j, 19:20], xt[:, j], ALU.mult, ALU.add).then_inc(s["y"], 1)

            with dve.Fori(0, NI) as i:
                n, turn = tiles(dve, i), dve.snap(i + 1)
                for stage in (norm, quantise):
                    for j in range(PAIR):
                        stage(j, n, turn)
                for j in range(PAIR):
                    products(i, j)
                for stage in (subln, quantise2, residual):
                    for j in range(PAIR):
                        stage(j, n, turn)

        @block.tensor
        def _(pe):
            pe.wait_ge(s["w_ternary"], 3)
            wg, wu = (wb[:, m].rearrange("p (c o) -> p c o", c=DC) for m in (0, 1))
            wd = wb[:, 2].rearrange("p (c o) -> p c o", c=FC)
            with pe.Fori(0, NI) as i:
                n = tiles(pe, i)

                def turn_x(j):
                    pe.wait_ge(s["quantised"], n[j])
                    for ic in range(DC):
                        last = nc.tensor.transpose(MB[:, j, ic * P:(ic + 1) * P], xq[:, j, ic * P:(ic + 1) * P], k["ident_b"][:])
                    last.then_inc(s["xT_psum"], 1)

                def gate_up(j):
                    pe.wait_ge(s["xT"], n[j])
                    for c in range(CH):
                        q = j * CH + c
                        pe.wait_ge(s["act_part"], i * SEQ + (q + 1))
                        for bank, wt_, sem in ((GB, wg, "g_psum"), (UB, wu, "u_psum")):
                            for ic in range(DC):
                                last = nc.tensor.matmul(bank[:, q % 2], xT[:, j, ic], wt_[:, ic, c * HALF:(c + 1) * HALF], start=ic == 0, stop=ic == DC - 1)
                            last.then_inc(s[sem], 1)

                def turn_h(j):
                    pe.wait_ge(s["quantised2"], n[j])
                    for c in range(FC):
                        last = nc.tensor.transpose(TP[:, j, c], hq[:, j, c * P:(c + 1) * P], k["ident_b"][:])
                    last.then_inc(s["hT_psum"], 1)

                def down(j):
                    pe.wait_ge(s["hT"], n[j])
                    for c in range(FC):
                        last = nc.tensor.matmul(M[:, j, 0:D], hT[:, j, c], wd[:, c], start=c == 0, stop=c == FC - 1)
                    last.then_inc(s["y_psum"], 1)

                pe.wait_ge(s["y"], i * PAIR + 1)
                for stage in (turn_x, gate_up, turn_h, down):
                    for j in range(PAIR):
                        stage(j)
    end_phase(nc, s)


def xatt2(nc, k, x_in, x_out, ctx_T, arena, load_next):
    GROUPS = 2 + 4
    SEQ = PAIR * GROUPS
    with ExitStack() as ctx:
        def sb(name, shape, dt=F32):
            return ctx.enter_context(nc.sbuf_tensor("xatt2_" + name, shape, dt))

        def w(name):
            return part(arena, W_XATT2, name)

        s = semaphores(nc, ctx, "xatt2_", """
            padded weights_next x_loaded0 x_loaded1 c_loaded0 c_loaded1 stored0 stored1 stats mean var rstd normed biased kept
            xT_psum xT qk_psum qk squares summed ms_eps rms qk_rms qk_scaled v_psum v
            turned evacuated s_psum row_max shifted exped o_psum denom o_norm oT_psum oT y_psum y""")
        S = k["psum"][:, 0:4, :].rearrange("p g (c m) -> p g c m", c=4)
        TP = k["psum"][:, 4:6, :].rearrange("p r (c m) -> p r c m", c=4)
        V = k["psum"][:, 4:6, :]
        M = k["psum"][:, 6:8, :]
        bqk = arena[:, 4 * DC * D:4 * DC * D + 2 * D]
        nqk = arena[:, 4 * DC * D + 4 * D:4 * DC * D + 6 * D]
        one = sb("one", [P, 1])
        xt = sb("xt", [P, PAIR, D])
        ct = sb("ct", [P, PAIR, DC, P])
        st = sb("st", [P, PAIR, 6])
        mv = sb("mv", [P, PAIR, 2])
        sm = sb("sm", [P, PAIR, 8])
        xn = sb("xn", [P, PAIR, D])
        xb = sb("xb", [P, PAIR, D])
        xr = sb("xr", [P, PAIR, D])
        xT = sb("xT", [P, PAIR, DC, P])
        qk = sb("qk", [P, PAIR, 2 * D])
        sq = sb("sq", [P, PAIR, 2 * D])
        qkp = sb("qkp", [P, PAIR, 2 * NH, 32])
        qkT = sb("qkT", [P, PAIR, 2, 4, P])
        v = sb("v", [P, PAIR, NH, HD + 1])
        mx = sb("mx", [P, PAIR, 4, 4])
        pr = sb("pr", [P, PAIR, 4, 4, P])
        pT = sb("pT", [P, PAIR, 4, 4, P])
        rd = sb("rd", [P, PAIR, NH])
        o = sb("o", [P, PAIR, D])
        oT = sb("oT", [P, PAIR, DC, P])
        y = sb("y", [P, PAIR, D])
        block = ctx.enter_context(nc.Block())

        @block.sync
        def _(sp):
            def load(t):
                for j in range(PAIR):
                    sp.wait_ge(s["v"], t * PAIR + 1)
                    sp.wait_ge(s["biased"], t * PAIR + 1)
                    sp.dma_start(ct[:, j], ctx_T[t * PAIR + j]).then_inc(s[f"c_loaded{j}"], 16)
                    sp.dma_start(xt[:, j], x_in[t * PAIR + j]).then_inc(s[f"x_loaded{j}"], 16)

            def store(t):
                m = tiles(sp, t)
                for j in range(PAIR):
                    sp.wait_ge(s["y"], m[j] + 1)
                    sp.dma_start(x_out[t * PAIR + j], y[:, j]).then_inc(s[f"stored{j}"], 16)

            start_next, finish_next = load_next
            loads_ahead(sp, load, store, lambda: start_next(sp, s["weights_next"]))
            for j in range(PAIR):
                sp.wait_ge(s[f"stored{j}"], (NI + 1) * 16)
            finish_next(sp, s["weights_next"])

        @block.gpsimd
        def _(pool):
            nc.gpsimd.memset(qkp[:], 0.0)
            nc.gpsimd.memset(v[:], 1.0)
            nc.gpsimd.memset(one[:], 1.0).then_inc(s["padded"], 1)

            def body(front, back):
                if front is not None:
                    n, turn = tiles(pool, front), front + 1
                    for j in range(PAIR):
                        pool.wait_ge(s["var"], n[j])
                        nc.gpsimd.tensor_tensor(sm[:, j, 1:2], sm[:, j, 0:1], k["neg_half"][:], ALU.pow).then_inc(s["rstd"], 1)
                    for j in range(PAIR):
                        pool.wait_ge(s[f"x_loaded{j}"], turn * 16)
                        pool.wait_ge(s["kept"], n[j])
                        nc.gpsimd.tensor_tensor(xb[:, j], xt[:, j], w("bo"), ALU.add).then_inc(s["biased"], 1)
                    for j in range(PAIR):
                        pool.wait_ge(s["ms_eps"], n[j])
                        nc.gpsimd.tensor_tensor(sm[:, j, 6:8], sm[:, j, 4:6], k["neg_half"][:].to_broadcast([P, 2]), ALU.pow).then_inc(s["rms"], 1)
                    for j in range(PAIR):
                        if back is not None:
                            pool.wait_ge(s["y"], n[j] - 1)
                        pool.wait_ge(s["biased"], n[j] + 1)
                        nc.gpsimd.tensor_tensor(xr[:, j], xb[:, j], one[:].to_broadcast([P, D]), ALU.mult).then_inc(s["kept"], 1)

            overlapped(pool, body)

        @block.scalar
        def _(act):
            def turned_x(j, n, turns):
                act.wait_ge(s["xT_psum"], n[j])
                nc.scalar.copy(xT[:, j], M[:, j, 0:DC * P]).then_inc(s["xT"], 1)

            def squares(j, n, turns):
                act.wait_ge(s["qk"], n[j])
                nc.scalar.activation(sq[:, j], qk[:, j], ACT.Square).then_inc(s["squares"], 1)

            def evacuate(dst, q, turns):
                act.wait_ge(s["turned"], (turns - 1) * SEQ + (q + 1))
                nc.scalar.copy(dst, TP[:, q % 2]).then_inc(s["evacuated"], 1)

            def turned_qk(j, n, turns):
                for g in range(2):
                    evacuate(qkT[:, j, g], 2 * j + g, turns)

            def exp(j, n, turns):
                act.wait_ge(s["shifted"], n[j] + 1)
                nc.scalar.activation(pr[:, j], pr[:, j], ACT.Exp, scale=HD ** -0.5).then_inc(s["exped"], 1)

            def turned_p(j, n, turns):
                for g in range(4):
                    evacuate(pT[:, j, g], 2 * PAIR + 4 * j + g, turns)

            def turned_o(j, n, turns):
                act.wait_ge(s["oT_psum"], n[j])
                nc.scalar.copy(oT[:, j], M[:, j, 0:DC * P]).then_inc(s["oT"], 1)

            def body(front, back):
                f, b = halves(act, front, back)
                f(turned_x, 0, 1)
                for j in range(PAIR):
                    b(exp, j)
                    f(squares, j)
                    b(turned_p, j)
                f(turned_qk, 0, 1)
                b(turned_o, 0, 1)

            overlapped(act, body)

        @block.vector
        def _(dve):
            credit(nc, k, s, y=1, v=1, biased=1, kept=2, shifted=1, evacuated=2, stored0=16, stored1=16)
            dve.wait_ge(s["padded"], 1)

            def norm(j, n, turn):
                dve.wait_ge(s[f"x_loaded{j}"], turn * 16)
                nc.vector.bn_stats(st[:, j], xt[:, j]).then_inc(s["stats"], 1)
                hold(dve, k["scratch"][:, j:j + 1], s["stats"], n[j])
                nc.vector.bn_aggr(mv[:, j], st[:, j]).then_inc(s["mean"], 1)
                dve.wait_ge(s["mean"], n[j])
                nc.vector.tensor_scalar(sm[:, j, 0:1], mv[:, j, 1:2], 1e-5, None, ALU.add).then_inc(s["var"], 1)

            def scaled(j, n, turn):
                dve.wait_ge(s["rstd"], n[j])
                nc.vector.tensor_scalar(xn[:, j], xt[:, j], mv[:, j, 0:1], sm[:, j, 1:2], ALU.subtract, ALU.mult).then_inc(s["normed"], 1)

            def bias(j, n, turn):
                dve.wait_ge(s["qk_psum"], n[j])
                nc.vector.tensor_tensor(qk[:, j], M[:, j], bqk, ALU.add).then_inc(s["qk"], 1)

            def values(j, n, turn):
                dve.wait_ge(s["v_psum"], n[j])
                nc.vector.tensor_tensor(v[:, j, :, 0:HD], V[:, j, 0:D].rearrange("p (h d) -> p h d", d=HD),
                                        w("bv").rearrange("p (h d) -> p h d", d=HD), ALU.add).then_inc(s["v"], 1)

            def sums(j, n, turn):
                dve.wait_ge(s["squares"], n[j])
                nc.vector.tensor_reduce(sm[:, j, 2:4], sq[:, j].rearrange("p (q d) -> p q d", q=2), X, ALU.add).then_inc(s["summed"], 1)
                dve.wait_ge(s["summed"], n[j])
                nc.vector.tensor_scalar(sm[:, j, 4:6], sm[:, j, 2:4], 1.0 / D, 1e-6, ALU.mult, ALU.add).then_inc(s["ms_eps"], 1)

            def rms(j, n, turn):
                dve.wait_ge(s["rms"], n[j])
                for m in range(2):
                    last = nc.vector.tensor_scalar(qk[:, j, m * D:(m + 1) * D], qk[:, j, m * D:(m + 1) * D], sm[:, j, 6 + m:7 + m], None, ALU.mult)
                last.then_inc(s["qk_rms"], 1)
                dve.wait_ge(s["qk_rms"], n[j])
                nc.vector.tensor_tensor(qkp[:, j, :, 0:HD], qk[:, j].rearrange("p (h d) -> p h d", d=HD),
                                        nqk.rearrange("p (h d) -> p h d", d=HD), ALU.mult).then_inc(s["qk_scaled"], 1)

            def softmax(j, n, turn):
                dve.wait_ge(s["s_psum"], n[j])
                nc.vector.tensor_reduce(mx[:, j], S, X, ALU.max).then_inc(s["row_max"], 1)
                dve.wait_ge(s["row_max"], n[j])
                for g in range(4):
                    last = nc.vector.tensor_tensor(pr[:, j, g], S[:, g], mx[:, j, g].unsqueeze(2).to_broadcast([P, 4, P]), ALU.subtract)
                last.then_inc(s["shifted"], 1)

            def output(j, n, turn):
                O = M[:, j, 0:NH * (HD + 1)].rearrange("p (h d) -> p h d", h=NH)
                dve.wait_ge(s["o_psum"], n[j])
                nc.vector.reciprocal(rd[:, j], O[:, :, HD]).then_inc(s["denom"], 1)
                dve.wait_ge(s["denom"], n[j])
                nc.vector.tensor_tensor(o[:, j].rearrange("p (h d) -> p h d", h=NH), O[:, :, 0:HD],
                                        rd[:, j].unsqueeze(2).to_broadcast([P, NH, HD]), ALU.mult).then_inc(s["o_norm"], 1)

            def residual(j, n, turn):
                dve.wait_ge(s["y_psum"], n[j])
                dve.wait_ge(s["kept"], n[j] + 2)
                dve.wait_ge(s[f"stored{j}"], turn * 16)
                nc.vector.tensor_tensor(y[:, j], M[:, j, 0:D], xr[:, j], ALU.add).then_inc(s["y"], 1)

            def body(front, back):
                f, b = halves(dve, front, back)
                f(norm, 0, 1)
                f(scaled, 0, 1)
                for j in range(PAIR):
                    b(softmax, j)
                    f(bias, j)
                f(sums, 0, 1)
                f(rms, 0, 1)
                b(output, 0)
                f(values, 0, 1)
                b(output, 1)
                b(residual, 0, 1)

            overlapped(dve, body)

        @block.tensor
        def _(pe):
            wq, wk, wv, wo = (w(m).rearrange("p (c o) -> p c o", c=DC) for m in ("wq", "wk", "wv", "wo"))
            def turn_x(j, n, turns):
                pe.wait_ge(s["normed"], n[j])
                for ic in range(DC):
                    last = nc.tensor.transpose(M[:, j, ic * P:(ic + 1) * P], xn[:, j, ic * P:(ic + 1) * P], k["ident"][:])
                last.then_inc(s["xT_psum"], 1)

            def queries_keys(j, n, turns):
                pe.wait_ge(s[f"c_loaded{j}"], turns * 16)
                pe.wait_ge(s["xT"], n[j])
                for m, (src, wt) in enumerate(((xT, wq), (ct, wk))):
                    for ic in range(DC):
                        last = nc.tensor.matmul(M[:, j, m * D:(m + 1) * D], src[:, j, ic], wt[:, ic], start=ic == 0, stop=ic == DC - 1)
                last.then_inc(s["qk_psum"], 1)

            def values(j, n, turns):
                for ic in range(DC):
                    last = nc.tensor.matmul(V[:, j, 0:D], ct[:, j, ic], wv[:, ic], start=ic == 0, stop=ic == DC - 1)
                last.then_inc(s["v_psum"], 1)

            def turn(q, turns, blocks):
                pe.wait_ge(s["evacuated"], (turns - 1) * SEQ + (q + 1))
                for c, b in enumerate(blocks):
                    last = nc.tensor.transpose(TP[:, q % 2, c], b, k["ident"][:])
                last.then_inc(s["turned"], 1)

            def turn_qk(j, n, turns):
                pe.wait_ge(s["qk_scaled"], n[j])
                if j == 0:
                    pe.wait_ge(s["v"], n[1] + 1)
                for g in range(2):
                    turn(2 * j + g, turns, [qkp[:, j, NH * g + 4 * c:NH * g + 4 * c + 4].rearrange("p h d -> p (h d)") for c in range(4)])

            def scores(j, n, turns):
                pe.wait_ge(s["evacuated"], (turns - 1) * SEQ + (2 * j + 4))
                pe.wait_ge(s["shifted"], n[j])
                for c in range(4):
                    for g in range(4):
                        r = slice(32 * g, 32 * g + 32)
                        last = nc.tensor.matmul(S[:, g, c], qkT[r, j, 0, c], qkT[r, j, 1, c], start=True, stop=True)
                last.then_inc(s["s_psum"], 1)

            def turn_p(j, n, turns):
                pe.wait_ge(s["exped"], n[j])
                for g in range(4):
                    turn(2 * PAIR + 4 * j + g, turns, [pr[:, j, g, c] for c in range(4)])

            def attend(j, n, turns):
                O = M[:, j, 0:NH * (HD + 1)].rearrange("p (h d) -> p h d", h=NH)
                pe.wait_ge(s["v"], n[j] + 1)
                pe.wait_ge(s["evacuated"], (turns - 1) * SEQ + (2 * PAIR + 4 * j + 6))
                for c in range(4):
                    for g in range(4):
                        last = nc.tensor.matmul(O[:, 4 * c + g], pT[:, j, g, c], v[:, j, 4 * c + g], start=True, stop=True)
                last.then_inc(s["o_psum"], 1)

            def turn_o(j, n, turns):
                pe.wait_ge(s["o_norm"], n[j])
                for ic in range(DC):
                    last = nc.tensor.transpose(M[:, j, ic * P:(ic + 1) * P], o[:, j, ic * P:(ic + 1) * P], k["ident"][:])
                last.then_inc(s["oT_psum"], 1)

            def project(j, n, turns):
                pe.wait_ge(s["oT"], n[j])
                for ic in range(DC):
                    last = nc.tensor.matmul(M[:, j, 0:D], oT[:, j, ic], wo[:, ic], start=ic == 0, stop=ic == DC - 1)
                last.then_inc(s["y_psum"], 1)

            def body(front, back):
                f, b = halves(pe, front, back)
                b(scores, 0)
                if back is not None:
                    pe.wait_ge(s["y"], back * PAIR + 1)
                f(turn_x, 0, 1)
                f(queries_keys, 0)
                b(scores, 1)
                b(turn_p, 0)
                f(queries_keys, 1)
                b(turn_p, 1)
                if front is not None:
                    pe.wait_ge(s["qk"], (front + 1) * PAIR)
                b(attend, 0, 1)
                f(values, 0, 1)
                f(turn_qk, 0, 1)
                b(turn_o, 0, 1)
                b(project, 0, 1)

            overlapped(pe, body)
    end_phase(nc, s)


def arrow(nc, k, x_in, x_out, arena, load_next):
    AC = AR * RR // P
    TOP = 4
    SEQ = PAIR * AC // 4
    with ExitStack() as ctx:
        def sb(name, shape, dt=F32):
            return ctx.enter_context(nc.sbuf_tensor("arrow_" + name, shape, dt))

        def w(name):
            return part(arena, W_ARROW, name)

        s = semaphores(nc, ctx, "arrow_", """
            tables weights_next x_loaded0 x_loaded1 stored0 stored1 stats mean var rstd normed biased xT_psum xT
            vecs_psum vecs squares norms root top above tied top2 pick thr sel route routed v outer
            turned evacuated linear_psum linear y_psum y""")
        V = k["psum"][:, 0:4, :].rearrange("p (j b) c -> p j (b c)", j=PAIR)
        TP = k["psum"][:, 4:6, :].rearrange("p r (c m) -> p r c m", c=4)
        M = k["psum"][:, 6:8, :]
        index = sb("index", [P, AR])
        count = sb("count", [P, TOP])
        xt = sb("xt", [P, PAIR, D])
        st = sb("st", [P, PAIR, 6])
        mv = sb("mv", [P, PAIR, 2])
        sm = sb("sm", [P, PAIR, 4])
        xn = sb("xn", [P, PAIR, D])
        xb = sb("xb", [P, PAIR, D])
        xr = sb("xr", [P, PAIR, D])
        xT = sb("xT", [P, PAIR, DC, P])
        vec = sb("vec", [P, PAIR, AR, RR])
        wk = sb("wk", [P, PAIR, AR, RR])
        outer = sb("outer", [P, PAIR, AR, RR])
        nr = sb("nr", [P, PAIR, 6, AR])
        t8 = sb("t8", [P, PAIR, 4, 8])
        vr = sb("vr", [P, PAIR, RR])
        uT = sb("uT", [P, PAIR, AC, P])
        y = sb("y", [P, PAIR, D])
        block = ctx.enter_context(nc.Block())

        @block.sync
        def _(sp):
            def load(t):
                for j in range(PAIR):
                    sp.wait_ge(s["normed"], t * PAIR + 1)
                    sp.wait_ge(s["biased"], t * PAIR + 1)
                    sp.dma_start(xt[:, j], x_in[t * PAIR + j]).then_inc(s[f"x_loaded{j}"], 16)

            def store(t):
                m = tiles(sp, t)
                for j in range(PAIR):
                    sp.wait_ge(s["y"], m[j] + 1)
                    sp.dma_start(x_out[t * PAIR + j], y[:, j]).then_inc(s[f"stored{j}"], 16)

            start_next, finish_next = load_next
            loads_ahead(sp, load, store, lambda: start_next(sp, s["weights_next"]))
            for j in range(PAIR):
                sp.wait_ge(s[f"stored{j}"], (NI + 1) * 16)
            finish_next(sp, s["weights_next"])

        @block.gpsimd
        def _(pool):
            nc.gpsimd.iota(index[:], pattern=[[-1, AR]], base=AR, channel_multiplier=0, allow_small_or_imprecise_dtypes=True)
            nc.gpsimd.iota(count[:], pattern=[[1, TOP]], base=1, channel_multiplier=0, allow_small_or_imprecise_dtypes=True).then_inc(s["tables"], 1)

            def body(front, back):
                if front is not None:
                    n, turn = tiles(pool, front), front + 1
                    for j in range(PAIR):
                        pool.wait_ge(s["var"], n[j])
                        nc.gpsimd.tensor_tensor(sm[:, j, 1:2], sm[:, j, 0:1], k["neg_half"][:], ALU.pow).then_inc(s["rstd"], 1)
                    for j in range(PAIR):
                        pool.wait_ge(s[f"x_loaded{j}"], turn * 16)
                        if back is not None:
                            pool.wait_ge(s["linear"], n[j] - 2)
                        nc.gpsimd.tensor_tensor(xb[:, j], xt[:, j], w("bias"), ALU.add).then_inc(s["biased"], 1)

            overlapped(pool, body)

        @block.scalar
        def _(act):
            def turned_x(j, n, turns):
                act.wait_ge(s["xT_psum"], n[j])
                nc.scalar.copy(xT[:, j], M[:, j, 0:DC * P]).then_inc(s["xT"], 1)

            def squares(j, n, turns):
                act.wait_ge(s["vecs_psum"], n[j])
                nc.scalar.copy(vec[:, j], V[:, j].rearrange("p (a r) -> p a r", r=RR)).then_inc(s["vecs"], 1)
                act.wait_ge(s["vecs"], n[j] + 1)
                nc.scalar.activation(wk[:, j], vec[:, j], ACT.Square).then_inc(s["squares"], 1)

            def root(j, n, turns):
                act.wait_ge(s["norms"], n[j])
                nc.scalar.activation(nr[:, j, 1], nr[:, j, 0], ACT.Sqrt).then_inc(s["root"], 1)

            def turned_u(j, n, turns):
                for g in range(AC // 4):
                    q = j * (AC // 4) + g
                    act.wait_ge(s["turned"], (turns - 1) * SEQ + (q + 1))
                    nc.scalar.copy(uT[:, j, 4 * g:4 * g + 4], TP[:, q % 2]).then_inc(s["evacuated"], 1)

            def body(front, back):
                f, b = halves(act, front, back)
                f(turned_x, 0, 1)
                f(squares, 0, 1)
                b(turned_u, 0, 1)
                f(root, 0, 1)

            overlapped(act, body)

        @block.vector
        def _(dve):
            credit(nc, k, s, y=1, normed=1, biased=1, vecs=1, evacuated=2, stored0=16, stored1=16)
            dve.wait_ge(s["tables"], 1)

            def norm(j, n, turn):
                dve.wait_ge(s[f"x_loaded{j}"], turn * 16)
                nc.vector.bn_stats(st[:, j], xt[:, j]).then_inc(s["stats"], 1)
                hold(dve, k["scratch"][:, j:j + 1], s["stats"], n[j])
                nc.vector.bn_aggr(mv[:, j], st[:, j]).then_inc(s["mean"], 1)
                dve.wait_ge(s["mean"], n[j])
                nc.vector.tensor_scalar(sm[:, j, 0:1], mv[:, j, 1:2], 1e-5, None, ALU.add).then_inc(s["var"], 1)

            def scaled(j, n, turn):
                dve.wait_ge(s["rstd"], n[j])
                nc.vector.tensor_scalar(xn[:, j], xt[:, j], mv[:, j, 0:1], sm[:, j, 1:2], ALU.subtract, ALU.mult).then_inc(s["normed"], 1)

            def norms(j, n, turn):
                dve.wait_ge(s["squares"], n[j])
                nc.vector.tensor_reduce(nr[:, j, 0], wk[:, j], X, ALU.add).then_inc(s["norms"], 1)

            def route(j, n, turn):
                norm_, above, tied, sel = (nr[:, j, m] for m in range(1, 5))
                best, best2, pick = t8[:, j, 0], t8[:, j, 1], t8[:, j, 2, 0:TOP]
                hold(dve, k["scratch"][:, 2 + j:3 + j], s["root"], n[j])
                nc.vector.max(best, norm_).then_inc(s["top"], 1)
                dve.wait_ge(s["top"], n[j])
                nc.vector.tensor_scalar(above, norm_, best[:, TOP - 1:TOP], 0.0, ALU.is_gt, ALU.add, accum_out=sm[:, j, 2:3]).then_inc(s["above"], 1)
                nc.vector.scalar_tensor_tensor(tied, norm_, best[:, TOP - 1:TOP], index[:], ALU.is_equal, ALU.mult).then_inc(s["tied"], 1)
                hold(dve, k["scratch"][:, 4 + j:5 + j], s["tied"], n[j])
                nc.vector.max(best2, tied).then_inc(s["top2"], 1)
                dve.wait_ge(s["above"], n[j])
                nc.vector.tensor_scalar(pick, count[:], sm[:, j, 2:3], float(TOP), ALU.add, ALU.is_equal).then_inc(s["pick"], 1)
                dve.wait_ge(s["pick"], n[j])
                dve.wait_ge(s["top2"], n[j])
                nc.vector.tensor_tensor_reduce(pick, pick, best2[:, 0:TOP], 1.0, 0.0, ALU.mult, ALU.add, sm[:, j, 3:4]).then_inc(s["thr"], 1)
                dve.wait_ge(s["thr"], n[j])
                nc.vector.scalar_tensor_tensor(sel, tied, sm[:, j, 3:4], above, ALU.is_ge, ALU.add).then_inc(s["sel"], 1)
                dve.wait_ge(s["sel"], n[j])
                nc.vector.tensor_scalar(nr[:, j, 5], sel, 1.0 / TOP, None, ALU.mult).then_inc(s["route"], 1)

            def combine(j, n, turn):
                dve.wait_ge(s["route"], n[j])
                r = nr[:, j, 5].unsqueeze(2).to_broadcast([P, AR, RR])
                nc.vector.tensor_tensor(wk[:, j], vec[:, j], r, ALU.mult).then_inc(s["routed"], 1)
                dve.wait_ge(s["routed"], n[j])
                nc.vector.tensor_reduce(vr[:, j], wk[:, j].rearrange("p a r -> p r a"), X, ALU.add).then_inc(s["v"], 1)
                dve.wait_ge(s["v"], n[j])
                nc.vector.tensor_tensor(outer[:, j], vr[:, j].unsqueeze(1).to_broadcast([P, AR, RR]), r, ALU.mult).then_inc(s["outer"], 1)

            def residual(j, n, turn):
                dve.wait_ge(s["y_psum"], n[j])
                dve.wait_ge(s["linear"], n[j])
                dve.wait_ge(s[f"stored{j}"], turn * 16)
                nc.vector.tensor_tensor(y[:, j], M[:, j, 0:D], xr[:, j], ALU.add).then_inc(s["y"], 1)

            def linear(j, n, turn):
                dve.wait_ge(s["linear_psum"], n[j])
                dve.wait_ge(s["biased"], n[j] + 1)
                nc.vector.tensor_tensor(xr[:, j], V[:, j, 0:D], xb[:, j], ALU.add).then_inc(s["linear"], 1)

            def body(front, back):
                f, b = halves(dve, front, back)
                f(norm, 0, 1)
                f(scaled, 0, 1)
                f(norms, 0, 1)
                f(route, 0, 1)
                b(residual, 0, 1)
                f(combine, 0, 1)
                f(linear, 0, 1)

            overlapped(dve, body)

        @block.tensor
        def _(pe):
            a, wt = (w(m).rearrange("p (c o) -> p c o", c=DC) for m in ("a", "w"))
            down = w("b").rearrange("p (c o) -> p c o", c=AC)
            def turn_x(j, n, turns):
                pe.wait_ge(s["normed"], n[j] + 1)
                for ic in range(DC):
                    last = nc.tensor.transpose(M[:, j, ic * P:(ic + 1) * P], xn[:, j, ic * P:(ic + 1) * P], k["ident"][:])
                last.then_inc(s["xT_psum"], 1)

            def vectors(j, n, turns):
                pe.wait_ge(s["xT"], n[j])
                pe.wait_ge(s["vecs"], (turns - 1) * PAIR + 1)
                for c in range(2):
                    for ic in range(DC):
                        last = nc.tensor.matmul(V[:, j, c * 512:(c + 1) * 512], xT[:, j, ic], a[:, ic, c * 512:(c + 1) * 512], start=ic == 0, stop=ic == DC - 1)
                last.then_inc(s["vecs_psum"], 1)

            def turn_u(j, n, turns):
                pe.wait_ge(s["outer"], n[j])
                for g in range(AC // 4):
                    q = j * (AC // 4) + g
                    pe.wait_ge(s["evacuated"], (turns - 1) * SEQ + (q + 1))
                    for c in range(4):
                        at = (4 * g + c) * P // RR
                        last = nc.tensor.transpose(TP[:, q % 2, c], outer[:, j, at:at + P // RR].rearrange("p a r -> p (a r)"), k["ident"][:])
                    last.then_inc(s["turned"], 1)

            def output(j, n, turns):
                pe.wait_ge(s["evacuated"], (turns - 1) * SEQ + ((j + 1) * (AC // 4) + 2))
                for c in range(AC):
                    last = nc.tensor.matmul(M[:, j, 0:D], uT[:, j, c], down[:, c], start=c == 0, stop=c == AC - 1)
                last.then_inc(s["y_psum"], 1)

            def linear(j, n, turns):
                pe.wait_ge(s["vecs"], n[j] + 1)
                for ic in range(DC):
                    last = nc.tensor.matmul(V[:, j, 0:D], xT[:, j, ic], wt[:, ic], start=ic == 0, stop=ic == DC - 1)
                last.then_inc(s["linear_psum"], 1)

            def body(front, back):
                f, b = halves(pe, front, back)
                if back is not None:
                    pe.wait_ge(s["y"], back * PAIR + 1)
                f(turn_x, 0, 1)
                if back is not None and front is not None:
                    pe.wait_ge(s["linear"], front * PAIR)
                f(vectors, 0, 1)
                b(turn_u, 0, 1)
                if front is not None:
                    pe.wait_ge(s["xT"], (front + 1) * PAIR)
                b(output, 0, 1)
                f(linear, 0, 1)

            overlapped(pe, body)
    end_phase(nc, s)


def qkv3(nc, k, x_in, ctx_T, qT_out, step_out, KT, vbuf, vmax, arena, load_next):
    W3 = 3 * 32
    with ExitStack() as ctx:
        def sb(name, shape, dt=F32):
            return ctx.enter_context(nc.sbuf_tensor("qkv3_" + name, shape, dt))

        def w(name):
            return part(arena, W_QKV3, name)

        s = semaphores(nc, ctx, "qkv3_", """
            padded weights_next x_loaded0 x_loaded1 c_loaded0 c_loaded1 q_stored0 q_stored1 s_stored0 s_stored1
            k_stored0 k_stored1 v_stored0 v_stored1 stats mean var rstd normed xT_psum xT qk_psum qk amax steps recip
            divided rounded q_step q_copied kq k_hi k_r1 k_mid k_r2 k_lo v_psum v vpos vmax qT_psum qT kT_psum kT""")
        bank = lambda a: k["psum"][:, a:a + 2, :].rearrange("p j c -> p (j c)").bitcast(BF16)
        QP = k["psum"][:, 0:4, :].rearrange("p j c -> p (j c)").bitcast(BF16).rearrange("p (j h m) -> p j h m", j=PAIR, h=NH)
        KP = bank(4).rearrange("p (j h m) -> p j h m", j=PAIR, h=NH // 2)
        M = k["psum"][:, 6:8, :]
        bqk = arena[:, 3 * DC * D:3 * DC * D + 2 * D]
        xt = sb("xt", [P, PAIR, D])
        ct = sb("ct", [P, PAIR, DC, P])
        st = sb("st", [P, PAIR, 6])
        mv = sb("mv", [P, PAIR, 2])
        sm = sb("sm", [P, PAIR, 2])
        xn = sb("xn", [P, PAIR, D])
        xT = sb("xT", [P, PAIR, DC, P])
        qk = sb("qk", [P, PAIR, 2 * NH, HD])
        stp = sb("stp", [P, PAIR, 3, 2 * NH])
        sq = sb("sq", [P, PAIR, NH])
        r1 = sb("r1", [P, PAIR, NH // 2, 32])
        Qp = sb("Qp", [P, PAIR, NH // 2, 2, 3, 32], BF16)
        Kp = sb("Kp", [P, PAIR, NH // 2, 3, 32], BF16)
        vs = sb("vs", [P, PAIR, D])
        qT = sb("qT", [W3, PAIR, NH, P], BF16)
        kT = sb("kT", [W3, PAIR, NH // 2, P], BF16)
        block = ctx.enter_context(nc.Block())

        @block.sync
        def _(sp):
            with sp.Fori(0, NI) as i:
                n, turn = tiles(sp, i), sp.snap(i + 1)
                for j in range(PAIR):
                    sp.wait_ge(s["v"], i * PAIR + 1)
                    sp.wait_ge(s["normed"], i * PAIR + 1)
                    sp.dma_start(ct[:, j], ctx_T[i * PAIR + j]).then_inc(s[f"c_loaded{j}"], 16)
                    sp.dma_start(xt[:, j], x_in[i * PAIR + j]).then_inc(s[f"x_loaded{j}"], 16)
                for j in range(PAIR):
                    sp.wait_ge(s["v"], n[j] + 1)
                    sp.dma_start(vbuf[:, i * PAIR + j], vs[:, j]).then_inc(s[f"v_stored{j}"], 16)
                for j in range(PAIR):
                    sp.wait_ge(s["kT"], n[j])
                    sp.dma_start(KT[:, i * PAIR + j], kT[:, j]).then_inc(s[f"k_stored{j}"], 16)
            for j in range(PAIR):
                sp.wait_ge(s[f"v_stored{j}"], (NI + 1) * 16)
                sp.wait_ge(s[f"k_stored{j}"], (NI + 1) * 16)
            for step in load_next:
                step(sp, s["weights_next"])

        @block.gpsimd
        def _(pool):
            nc.gpsimd.memset(Qp[:], 0.0).then_inc(s["padded"], 1)
            with pool.Fori(0, NI) as i:
                n = tiles(pool, i)
                for j in range(PAIR):
                    pool.wait_ge(s["var"], n[j])
                    nc.gpsimd.tensor_tensor(sm[:, j, 1:2], sm[:, j, 0:1], k["neg_half"][:], ALU.pow).then_inc(s["rstd"], 1)

        @block.scalar
        def _(act):
            with act.Fori(0, NI) as i:
                n, turn = tiles(act, i), act.snap(i + 1)

                def turned_x(j):
                    act.wait_ge(s["xT_psum"], n[j])
                    nc.scalar.copy(xT[:, j], M[:, j, 0:DC * P]).then_inc(s["xT"], 1)

                def turned_k(j):
                    act.wait_ge(s["kT_psum"], n[j])
                    act.wait_ge(s[f"k_stored{j}"], turn * 16)
                    nc.scalar.copy(kT[:, j], KP[0:W3, j]).then_inc(s["kT"], 1)

                def turned_q(j):
                    act.wait_ge(s["qT_psum"], n[j])
                    act.wait_ge(s[f"q_stored{j}"], turn * 16)
                    nc.scalar.copy(qT[:, j, 0:NH // 2], QP[0:W3, j, 0:NH // 2])
                    nc.scalar.copy(qT[:, j, NH // 2:], QP[0:W3, j, NH // 2:]).then_inc(s["qT"], 1)

                def store(j):
                    act.wait_ge(s["q_step"], n[j])
                    act.dma_start(step_out[i * PAIR + j], sq[:, j]).then_inc(s[f"s_stored{j}"], 16)
                    act.wait_ge(s["qT"], n[j])
                    act.dma_start(qT_out[i * PAIR + j], qT[:, j].rearrange("p h m -> p (h m)")).then_inc(s[f"q_stored{j}"], 16)

                for stage in (turned_x, turned_q, turned_k, store):
                    for j in range(PAIR):
                        stage(j)
            for j in range(PAIR):
                act.wait_ge(s[f"s_stored{j}"], (NI + 1) * 16)
                act.wait_ge(s[f"q_stored{j}"], (NI + 1) * 16)

        @block.vector
        def _(dve):
            credit(nc, k, s, v=1, normed=1, **{f"{m}_stored{j}": 16 for m in "qskv" for j in range(PAIR)})
            nc.vector.memset(vmax[:], 0.0).then_inc(s["vmax"], 1)
            dve.wait_ge(s["padded"], 1)

            def norm(j, n, turn):
                dve.wait_ge(s[f"x_loaded{j}"], turn * 16)
                nc.vector.bn_stats(st[:, j], xt[:, j]).then_inc(s["stats"], 1)
                hold(dve, k["scratch"][:, j:j + 1], s["stats"], n[j])
                nc.vector.bn_aggr(mv[:, j], st[:, j]).then_inc(s["mean"], 1)
                dve.wait_ge(s["mean"], n[j])
                nc.vector.tensor_scalar(sm[:, j, 0:1], mv[:, j, 1:2], 1e-5, None, ALU.add).then_inc(s["var"], 1)

            def scaled(j, n, turn):
                dve.wait_ge(s["rstd"], n[j])
                nc.vector.tensor_scalar(xn[:, j], xt[:, j], mv[:, j, 0:1], sm[:, j, 1:2], ALU.subtract, ALU.mult).then_inc(s["normed"], 1)

            def bias(j, n, turn):
                dve.wait_ge(s["qk_psum"], n[j])
                nc.vector.tensor_tensor(qk[:, j], M[:, j].rearrange("p (h d) -> p h d", d=HD), bqk.rearrange("p (h d) -> p h d", d=HD), ALU.add).then_inc(s["qk"], 1)

            def quantise(j, n, turn):
                amax, step, inv = (stp[:, j, m] for m in range(3))
                dve.wait_ge(s["qk"], n[j])
                nc.vector.tensor_reduce(amax, qk[:, j], X, ALU.max, apply_absolute_value=True).then_inc(s["amax"], 1)
                dve.wait_ge(s["amax"], n[j])
                nc.vector.tensor_scalar(step[:, 0:NH], amax[:, 0:NH], 1.0 / 127.0, 1e-8 * HD ** 0.5, ALU.mult, ALU.max)
                nc.vector.tensor_scalar(step[:, NH:], amax[:, NH:], 1.0 / 127.0, 1e-8, ALU.mult, ALU.max).then_inc(s["steps"], 1)
                dve.wait_ge(s["steps"], n[j])
                nc.vector.reciprocal(inv, step).then_inc(s["recip"], 1)
                dve.wait_ge(s[f"s_stored{j}"], turn * 16)
                nc.vector.tensor_scalar(sq[:, j], step[:, 0:NH], HD ** -0.5, None, ALU.mult).then_inc(s["q_step"], 1)
                dve.wait_ge(s["recip"], n[j])
                nc.vector.tensor_tensor(qk[:, j], qk[:, j], inv.unsqueeze(2).to_broadcast([P, 2 * NH, HD]), ALU.mult).then_inc(s["divided"], 1)
                dve.wait_ge(s["divided"], n[j])
                nc.vector.tensor_scalar(qk[:, j], qk[:, j], MAGIC, MAGIC, ALU.add, ALU.subtract).then_inc(s["rounded"], 1)

            def place_q(j, n, turn):
                dve.wait_ge(s["rounded"], n[j])
                for a in range(2):
                    src = qk[:, j, a:NH:2].unsqueeze(2).to_broadcast([P, NH // 2, 3, HD])
                    last = nc.vector.tensor_copy(Qp[:, j, :, a, :, HD * a:HD * a + HD], src)
                last.then_inc(s["q_copied"], 1)

            def split_k(j, n, turn):
                rest = r1[:, j]
                kh, km, kl = (Kp[:, j, :, m] for m in range(3))
                nc.vector.tensor_tensor(rest.rearrange("p q (a d) -> p (q a) d", a=2), qk[:, j, NH:], stp[:, j, 1, NH:].unsqueeze(2).to_broadcast([P, NH, HD]), ALU.mult).then_inc(s["kq"], 1)
                dve.wait_ge(s["kq"], n[j])
                nc.vector.tensor_copy(kh, rest).then_inc(s["k_hi"], 1)
                dve.wait_ge(s["k_hi"], n[j])
                nc.vector.tensor_tensor(rest, rest, kh, ALU.subtract).then_inc(s["k_r1"], 1)
                dve.wait_ge(s["k_r1"], n[j])
                nc.vector.tensor_copy(km, rest).then_inc(s["k_mid"], 1)
                dve.wait_ge(s["k_mid"], n[j])
                nc.vector.tensor_tensor(rest, rest, km, ALU.subtract).then_inc(s["k_r2"], 1)
                dve.wait_ge(s["k_r2"], n[j])
                nc.vector.tensor_copy(kl, rest).then_inc(s["k_lo"], 1)

            def values(j, n, turn):
                dve.wait_ge(s["v_psum"], n[j])
                dve.wait_ge(s[f"v_stored{j}"], turn * 16)
                nc.vector.tensor_tensor(vs[:, j], M[:, j, 0:D], w("bv"), ALU.add).then_inc(s["v"], 1)
                dve.wait_ge(s["v"], n[j] + 1)
                dve.wait_ge(s["vmax"], n[j])
                nc.vector.tensor_tensor(vmax[:], vmax[:], vs[:, j], ALU.max).then_inc(s["vpos"], 1)
                dve.wait_ge(s["vpos"], n[j])
                nc.vector.scalar_tensor_tensor(vmax[:], vs[:, j], -1.0, vmax[:], ALU.mult, ALU.max).then_inc(s["vmax"], 1)

            with dve.Fori(0, NI) as i:
                n, turn = tiles(dve, i), dve.snap(i + 1)
                for stage in (norm, scaled, bias, quantise, place_q, split_k, values):
                    for j in range(PAIR):
                        stage(j, n, turn)

        @block.tensor
        def _(pe):
            wq, wk, wv = (w(m).rearrange("p (c o) -> p c o", c=DC) for m in ("wq", "wk", "wv"))
            with pe.Fori(0, NI) as i:
                n, turn = tiles(pe, i), pe.snap(i + 1)

                def turn_x(j):
                    pe.wait_ge(s["normed"], n[j] + 1)
                    for ic in range(DC):
                        last = nc.tensor.transpose(M[:, j, ic * P:(ic + 1) * P], xn[:, j, ic * P:(ic + 1) * P], k["ident"][:])
                    last.then_inc(s["xT_psum"], 1)

                def queries_keys(j):
                    pe.wait_ge(s[f"c_loaded{j}"], turn * 16)
                    pe.wait_ge(s["xT"], n[j])
                    for m, (src, wt) in enumerate(((xT, wq), (ct, wk))):
                        for ic in range(DC):
                            last = nc.tensor.matmul(M[:, j, m * D:(m + 1) * D], src[:, j, ic], wt[:, ic], start=ic == 0, stop=ic == DC - 1)
                    last.then_inc(s["qk_psum"], 1)

                def values(j):
                    pe.wait_ge(s["qk"], n[j])
                    for ic in range(DC):
                        last = nc.tensor.matmul(M[:, j, 0:D], ct[:, j, ic], wv[:, ic], start=ic == 0, stop=ic == DC - 1)
                    last.then_inc(s["v_psum"], 1)

                def turn_q(j):
                    pe.wait_ge(s["q_copied"], n[j])
                    for h in range(NH):
                        last = nc.tensor.transpose(QP[0:W3, j, h], Qp[:, j, h // 2, h % 2].rearrange("p a c -> p (a c)"), k["ident_b"][:])
                    last.then_inc(s["qT_psum"], 1)

                def turn_k(j):
                    pe.wait_ge(s["k_lo"], n[j])
                    for h in range(NH // 2):
                        last = nc.tensor.transpose(KP[0:W3, j, h], Kp[:, j, h].rearrange("p a c -> p (a c)"), k["ident_b"][:])
                    last.then_inc(s["kT_psum"], 1)

                pe.wait_ge(s["v"], i * PAIR + 1)
                for stage in (turn_x, queries_keys, values, turn_q, turn_k):
                    for j in range(PAIR):
                        stage(j)
    end_phase(nc, s)


def attend3(nc, k, qT_in, step_in, out, KT, vbuf, vmax, load_next):
    W3 = 3 * 32
    UK = B * P // 2
    UC = UK // P
    UN = 2 * NH
    TU = PAIR * UN
    LAG = 4
    LN255 = 5.541263545158426
    with ExitStack() as ctx:
        def sb(name, shape, dt=F32):
            return ctx.enter_context(nc.sbuf_tensor("attend3_" + name, shape, dt))

        s = semaphores(nc, ctx, "attend3_", """
            weights_next q_loaded0 q_loaded1 s_loaded0 s_loaded1 o_stored0 o_stored1
            v_all v_step v_recip v_divided v_ready scores unit_max row_max neg_step bias exped rounded turned evacuated
            attended both row_recip probs_step scaled o_done""")
        S = k["psum"][:, 0:6, :].rearrange("p (u b) c -> p u (b c)", b=2)
        TP = k["psum"][:, 6, :].bitcast(BF16).rearrange("p (c m) -> p c m", m=P)
        O = k["psum"][:, 7, 0:D]
        va = sb("va", [P, 3, D])
        V = sb("V", [P, B, D], BF16)
        qt = sb("qt", [W3, PAIR, NH * P], BF16)
        sq = sb("sq", [P, PAIR, NH])
        ns = sb("ns", [P, PAIR, NH])
        mx = sb("mx", [P, PAIR, NH, 4])
        sums = sb("sums", [P, PAIR, 2, NH])
        tot = sb("tot", [P, PAIR, 3, NH])
        ex = sb("ex", [P, 4, UK])
        pq = sb("pq", [P, 4, UK], BF16)
        pT = sb("pT", [P, 4, UC, P], BF16)
        o = sb("o", [P, PAIR, D])
        block = ctx.enter_context(nc.Block())

        def slot(u):
            return (u % UN) % 3

        @block.sync
        def _(sp):
            def load(i, j):
                sp.dma_start(qt[:, j], qT_in[i * PAIR + j]).then_inc(s[f"q_loaded{j}"], 16)
                sp.dma_start(sq[:, j], step_in[i * PAIR + j]).then_inc(s[f"s_loaded{j}"], 16)

            def store(i, j):
                sp.wait_ge(s["o_done"], i * PAIR + (j + 1))
                sp.dma_start(out[i * PAIR + j], o[:, j]).then_inc(s[f"o_stored{j}"], 16)

            start_next, finish_next = load_next
            for j in range(PAIR):
                load(0, j)
            start_next(sp, s["weights_next"])
            with sp.Fori(1, NI) as i:
                for j in range(PAIR):
                    sp.wait_ge(s["exped"], i * TU + ((j + 1) * UN + 2 - TU))
                    load(i, j)
                    store(i - 1, j)
            for j in range(PAIR):
                store(NI - 1, j)
            for j in range(PAIR):
                sp.wait_ge(s[f"o_stored{j}"], (NI + 1) * 16)
            finish_next(sp, s["weights_next"])

        @block.gpsimd
        def _(pool):
            nc.gpsimd.partition_all_reduce(va[:, 0], vmax[:], P, RMAX).then_inc(s["v_all"], 1)

        @block.scalar
        def _(act):
            def exp(i, u):
                j, h = u // UN, u % UN // 2
                if u % 2 == 0:
                    act.wait_ge(s["bias"], i * (TU // 2) + (u // 2 + 1))
                act.wait_ge(s["rounded"], i * TU + (u + 1))
                nc.scalar.activation(ex[:, u % 4], S[:, slot(u)], ACT.Exp, bias=mx[:, j, h, 3:4], scale=sq[:, j, h:h + 1],
                                     accum_out=sums[:, j, u % 2, h:h + 1]).then_inc(s["exped"], 1)

            def turned(i, u):
                act.wait_ge(s["turned"], i * TU + (u + 5))
                nc.scalar.copy(pT[:, u % 4], TP).then_inc(s["evacuated"], 1)

            def body(i, first):
                for u in range(TU):
                    exp(i, u)
                    if u >= 2:
                        turned(i, u - 2)
                    elif not first:
                        turned(i - 1, TU - 2 + u)

            body(0, True)
            with act.Fori(1, NI) as i:
                body(i, False)
            turned(NI - 1, TU - 2)
            turned(NI - 1, TU - 1)

        @block.vector
        def _(dve):
            credit(nc, k, s, exped=2, rounded=4, evacuated=1, turned=4, scaled=1, o_stored0=16, o_stored1=16)
            dve.wait_ge(s["v_all"], 1)
            nc.vector.tensor_scalar(va[:, 1], va[:, 0], 1.0 / 127.0, 1e-8, ALU.mult, ALU.max).then_inc(s["v_step"], 1)
            dve.wait_ge(s["v_step"], 1)
            nc.vector.reciprocal(va[:, 2], va[:, 1]).then_inc(s["v_recip"], 1)
            dve.wait_ge(s["v_recip"], 1)
            nc.vector.tensor_tensor(vbuf[:], vbuf[:], va[:, 2].unsqueeze(1).to_broadcast([P, B, D]), ALU.mult).then_inc(s["v_divided"], 1)
            dve.wait_ge(s["v_divided"], 1)
            nc.vector.tensor_scalar(V[:], vbuf[:], MAGIC, MAGIC, ALU.add, ALU.subtract).then_inc(s["v_ready"], 1)

            def prepare(i, j):
                dve.wait_ge(s[f"s_loaded{j}"], i * 16 + 16)
                nc.vector.tensor_scalar(ns[:, j], sq[:, j], -1.0, None, ALU.mult).then_inc(s["neg_step"], 1)

            def maximum(i, u):
                j, h = u // UN, u % UN // 2
                dve.wait_ge(s["scores"], i * TU + (u + 1))
                nc.vector.tensor_reduce(mx[:, j, h, u % 2:u % 2 + 1], S[:, slot(u)], X, ALU.max).then_inc(s["unit_max"], 1)

            def bias(i, u):
                j, h = u // UN, u % UN // 2
                dve.wait_ge(s["unit_max"], i * TU + (u + 1))
                nc.vector.tensor_tensor(mx[:, j, h, 2:3], mx[:, j, h, 0:1], mx[:, j, h, 1:2], ALU.max).then_inc(s["row_max"], 1)
                if h == 0:
                    dve.wait_ge(s["neg_step"], i * PAIR + (j + 1))
                dve.wait_ge(s["row_max"], i * (TU // 2) + (u // 2 + 1))
                nc.vector.tensor_scalar(mx[:, j, h, 3:4], mx[:, j, h, 2:3], ns[:, j, h:h + 1], LN255, ALU.mult, ALU.add).then_inc(s["bias"], 1)

            def rounding(i, u):
                dve.wait_ge(s["exped"], i * TU + (u + 3))
                dve.wait_ge(s["turned"], i * TU + (u + 1))
                nc.vector.tensor_scalar(pq[:, u % 4], ex[:, u % 4], MAGIC, MAGIC, ALU.add, ALU.subtract).then_inc(s["rounded"], 1)

            def finish(i, j):
                t = i * PAIR + (j + 1)
                dve.wait_ge(s["exped"], i * TU + ((j + 1) * UN + 2))
                nc.vector.tensor_tensor(tot[:, j, 0], sums[:, j, 0], sums[:, j, 1], ALU.add).then_inc(s["both"], 1)
                dve.wait_ge(s["both"], t)
                nc.vector.reciprocal(tot[:, j, 1], tot[:, j, 0]).then_inc(s["row_recip"], 1)
                dve.wait_ge(s["row_recip"], t)
                nc.vector.tensor_scalar(tot[:, j, 2], tot[:, j, 1], 1e-8, None, ALU.max).then_inc(s["probs_step"], 1)
                dve.wait_ge(s["probs_step"], t)
                dve.wait_ge(s["attended"], i * TU + (j + 1) * UN)
                dve.wait_ge(s[f"o_stored{j}"], i * 16 + 16)
                nc.vector.tensor_tensor(o[:, j].rearrange("p (h d) -> p h d", d=HD), O.rearrange("p (h d) -> p h d", d=HD),
                                        tot[:, j, 2].unsqueeze(2).to_broadcast([P, NH, HD]), ALU.mult).then_inc(s["scaled"], 1)
                dve.wait_ge(s["scaled"], t + 1)
                nc.vector.tensor_tensor(o[:, j], o[:, j], va[:, 1], ALU.mult).then_inc(s["o_done"], 1)

            def body(i, first):
                for u in range(0, TU, 2):
                    j = u // UN
                    if u % UN == 0:
                        prepare(i, j)
                    earlier = (i, u - 2) if u >= 2 else None if first else (i - 1, TU - 2)
                    maximum(i, u)
                    if earlier:
                        rounding(*earlier)
                    maximum(i, u + 1)
                    bias(i, u + 1)
                    if u % UN == 4 and not (first and j == 0):
                        finish(*((i, j - 1) if j else (i - 1, PAIR - 1)))
                    if earlier:
                        rounding(earlier[0], earlier[1] + 1)

            body(0, True)
            with dve.Fori(1, NI) as i:
                body(i, False)
            rounding(NI - 1, TU - 2)
            rounding(NI - 1, TU - 1)
            finish(NI - 1, PAIR - 1)

        @block.tensor
        def _(pe):
            def score(i, u):
                j, h = u // UN, u % UN // 2
                v = u % UN
                if v == 0:
                    pe.wait_ge(s[f"q_loaded{j}"], i * 16 + 16)
                    pe.wait_ge(s["exped"], i * TU + (u + 1))
                elif v == 1:
                    pe.wait_ge(s["exped"], i * TU + (u + 1))
                elif v >= 3:
                    pe.wait_ge(s["exped"], i * TU + u)
                for b in range(2):
                    c = (u % 2) * UC + 4 * b
                    last = nc.tensor.matmul(S[:, slot(u), b * 512:(b + 1) * 512], qt[:, j, h * P:(h + 1) * P],
                                            KT[:, c:c + 4, h // 2], start=True, stop=True)
                last.then_inc(s["scores"], 1)

            def turn(i, u):
                pe.wait_ge(s["rounded"], i * TU + (u + 5))
                pe.wait_ge(s["evacuated"], i * TU + (u + 1))
                for c in range(UC):
                    last = nc.tensor.transpose(TP[:, c], pq[:, u % 4, c * P:(c + 1) * P], k["ident_b"][:])
                last.then_inc(s["turned"], 1)

            def attend(i, u):
                j, h = u // UN, u % UN // 2
                pe.wait_ge(s["evacuated"], i * TU + (u + 2))
                if u % UN == 0:
                    pe.wait_ge(s["scaled"], i * PAIR + (j + 1))
                for c in range(UC):
                    kc = (u % 2) * UC + c
                    last = nc.tensor.matmul(O[:, h * HD:(h + 1) * HD], pT[:, u % 4, c], V[:, kc, h * HD:(h + 1) * HD],
                                            start=kc == 0, stop=kc == B - 1)
                last.then_inc(s["attended"], 1)

            def body(i, first):
                for u in range(TU):
                    score(i, u)
                    if u >= LAG:
                        turn(i, u - LAG)
                    elif not first:
                        turn(i - 1, TU - LAG + u)
                    if u > LAG:
                        attend(i, u - LAG - 1)
                    elif not first:
                        attend(i - 1, TU - LAG - 1 + u)

            pe.wait_ge(s["v_ready"], 1)
            body(0, True)
            with pe.Fori(1, NI) as i:
                body(i, False)
            for u in range(LAG):
                turn(NI - 1, TU - LAG + u)
                attend(NI - 1, TU - LAG - 1 + u)
            attend(NI - 1, TU - 1)
    end_phase(nc, s)


def build(nc, x, ctx_T, out, packs):
    res = [nc.dram_tensor(f"residual{i}", [B, P, D], F32, kind="Internal").ap() for i in range(2)]
    hid = nc.dram_tensor("hidden", [B, P, D], F32, kind="Internal").ap()
    att = nc.dram_tensor("attended", [B, P, D], F32, kind="Internal").ap()
    qT = nc.dram_tensor("queries_turned", [B, 96, NH * P], BF16, kind="Internal").ap()
    q_step = nc.dram_tensor("query_steps", [B, P, NH], F32, kind="Internal").ap()
    with ExitStack() as ctx:
        ready = ctx.enter_context(nc.semaphore("constants_ready"))
        loaded = ctx.enter_context(nc.semaphore("first_weights"))
        size = [max(words(v) for v in (W_XATT0, W_MOE0, W_XATT2, W_QKV3)),
                max(words(v) for v in (W_GQA, W_BIT, W_ARROW, W_MOE3))]
        arena = [ctx.enter_context(nc.sbuf_tensor(f"arena{i}", [P, size[i]], F32)) for i in range(2)]
        psum = ctx.enter_context(nc.psum_tensor("psum", [P, 8, 512], F32))
        ident = ctx.enter_context(nc.sbuf_tensor("ident", [P, P], F32))
        ident_b = ctx.enter_context(nc.sbuf_tensor("ident_b", [P, P], BF16))
        neg_half = ctx.enter_context(nc.sbuf_tensor("neg_half", [P, 1], F32))
        scratch = ctx.enter_context(nc.sbuf_tensor("scratch", [P, 32], F32))
        k = dict(scratch=scratch, ready=ready, psum=psum, ident=ident, ident_b=ident_b, neg_half=neg_half)

        def loader(name, layout, a):
            def start(sp, sem):
                sp.dma_start(arena[a][:, 0:words(layout)], packs[name]).then_inc(sem, 16)

            def finish(sp, sem):
                sp.wait_ge(sem, 16)
            return start, finish

        nothing = ()

        with nc.Block() as block:
            @block.sync
            def _(sp):
                for step in loader("xatt0", W_XATT0, 0):
                    step(sp, loaded)

            @block.gpsimd
            def _(pool):
                nc.gpsimd.memset(neg_half[:], -0.5)
                nc.gpsimd.memset(ident[:], 0.0)
                nc.gpsimd.memset(ident_b[:], 0.0).then_inc(ready, 1)
                pool.wait_ge(ready, 1)
                for m in (ident, ident_b):
                    nc.gpsimd.affine_select(out=m[:], in_=m[:], compare_op=ALU.not_equal, fill=1.0, base=0,
                                            pattern=[[-1, P]], channel_multiplier=1).then_inc(ready, 1)
        xatt0(nc, k, x["x"], res[0], ctx_T, arena[0], loader("gqa", W_GQA, 1))
        gqa(nc, k, res[0], hid, arena[1], loader("moe0", W_MOE0, 0))
        moe(nc, k, W_MOE0, res[0], hid, res[1], arena[0], loader("bit", W_BIT, 1))
        xmask(nc, k, res[1], res[0], ctx_T, x["ctx"], x["mask"], nothing)
        bit(nc, k, res[0], res[1], arena[1], loader("xatt2", W_XATT2, 0))
        xatt2(nc, k, res[1], res[0], ctx_T, arena[0], loader("arrow", W_ARROW, 1))
        arrow(nc, k, res[0], res[1], arena[1], loader("qkv3", W_QKV3, 0))
        with ExitStack() as kept:
            KT = kept.enter_context(nc.sbuf_tensor("keys_turned", [96, B, NH // 2, P], BF16))
            vbuf = kept.enter_context(nc.sbuf_tensor("values", [P, B, D], F32))
            vmax = kept.enter_context(nc.sbuf_tensor("values_max", [P, D], F32))
            qkv3(nc, k, res[1], ctx_T, qT, q_step, KT, vbuf, vmax, arena[0], nothing)
            attend3(nc, k, qT, q_step, att, KT, vbuf, vmax, loader("moe3", W_MOE3, 1))
        moe(nc, k, W_MOE3, res[1], att, out, arena[1], nothing)


_NAMES = ["xatt0", "gqa", "moe0", "bit", "xatt2", "arrow", "qkv3", "moe3"]


def kernel(**inputs):
    import numpy as np
    import concourse.bacc as bacc
    from concourse.bass_utils import run_bass_kernel_spmd as run

    a = {n: np.asarray(v) for n, v in inputs.items()}

    def cols(w):
        w = np.asarray(w)
        return np.ascontiguousarray(w.reshape(w.shape[0] // P, P, w.shape[1]).transpose(1, 0, 2)).reshape(P, -1)

    def row(v):
        return np.broadcast_to(np.asarray(v).reshape(1, -1), (P, v.size))

    def heads32(v):
        z = np.zeros(v.shape[:-1] + (NH, 32), v.dtype)
        z[..., :HD] = v.reshape(v.shape[:-1] + (NH, HD))
        return z.reshape(v.shape[:-1] + (NH * 32,))

    def pack(layout, parts):
        for n, size in layout.items():
            assert parts[n].shape == (P, size), (n, parts[n].shape, size)
        return np.ascontiguousarray(np.concatenate([parts[n] for n in layout], axis=1))

    g = lambda n: a[n]
    packs, layouts = {}, {}
    wkv, bkv = g("L0_xattn_wkv"), g("L0_xattn_bkv")
    layouts["xatt0"] = W_XATT0
    packs["xatt0"] = dict(
        wq=cols(g("L0_xattn_wq")), wp=cols(g("L0_xattn_wp")), wk=cols(heads32(wkv[:D].T)), wv=cols(wkv[D:].T),
        bq=heads32(g("L0_xattn_bq")).reshape(4, P).T, bk=heads32(bkv[:D]).reshape(4, P).T,
        bv=row(bkv[D:]), bp=row(g("L0_xattn_bp")))
    freqs = 1.0 / 1000000.0 ** (np.arange(0, GD, 2, dtype=np.float32) / np.float32(GD))
    angle = np.outer(np.arange(P, dtype=np.float32), freqs.astype(np.float32))
    layouts["gqa"] = W_GQA
    packs["gqa"] = dict(
        wq=cols(g("L0_ffn_q_w").T), wk=cols(g("L0_ffn_k_w").T), wv=cols(g("L0_ffn_v_w").T), wo=cols(g("L0_ffn_o_w").T),
        norm=row(g("L0_ffn_attn_norm_w")), qn=row(g("L0_ffn_q_norm_w")), kn=row(g("L0_ffn_k_norm_w")),
        cos=np.cos(angle).astype(np.float32), sin=np.sin(angle).astype(np.float32))
    side = lambda w: w.reshape(-1, D).T
    layouts["moe0"] = W_MOE0
    packs["moe0"] = dict(
        gate=cols(g("L0_ffn_gate_w").T), wg=cols(side(g("L0_ffn_wg"))), wu=cols(side(g("L0_ffn_wu"))),
        wd=cols(g("L0_ffn_wd").transpose(0, 2, 1).reshape(EI, D)), norm=row(g("L0_ffn_ffn_norm_w")))
    layouts["bit"] = W_BIT
    packs["bit"] = dict(wg=cols(g("L1_ffn_w_gate").T), wu=cols(g("L1_ffn_w_up").T), wd=cols(g("L1_ffn_w_down").T),
                        g=row(g("L1_ffn_subln_weight")))
    layouts["xatt2"] = W_XATT2
    packs["xatt2"] = dict(
        wq=cols(g("L2_xattn_q_w").T), wk=cols(g("L2_xattn_k_img_w").T), wv=cols(g("L2_xattn_v_img_w").T),
        wo=cols(g("L2_xattn_o_w").T), bq=row(g("L2_xattn_q_b")), bk=row(g("L2_xattn_k_img_b")),
        bv=row(g("L2_xattn_v_img_b")), bo=row(g("L2_xattn_o_b")), nq=row(g("L2_xattn_norm_q_w")),
        nk=row(g("L2_xattn_norm_k_img_w")))
    layouts["arrow"] = W_ARROW
    packs["arrow"] = dict(
        a=cols(g("L2_ffn_A").reshape(AR * RR, D).T), b=cols(g("L2_ffn_B").transpose(0, 2, 1).reshape(AR * RR, D)),
        w=cols(g("L2_ffn_W").T), bias=row(g("L2_ffn_bias")))
    w3, b3 = g("L3_xattn_Wkv"), g("L3_xattn_bkv")
    layouts["qkv3"] = W_QKV3
    packs["qkv3"] = dict(wq=cols(g("L3_xattn_Wq")), wk=cols(w3[:, :D]), wv=cols(w3[:, D:]), bq=row(g("L3_xattn_bq")),
                         bk=row(b3[:D]), bv=row(b3[D:]))
    both = lambda e, sh: np.concatenate([e, sh], axis=0)
    down = np.zeros((DN3 * P, D), np.float32)
    down[:GU3] = both(g("L3_ffn_expert_down").transpose(0, 2, 1).reshape(EI, D), g("L3_ffn_shared_down").T)
    layouts["moe3"] = W_MOE3
    packs["moe3"] = dict(
        wp=cols(g("L3_xattn_Wp")), bp=row(g("L3_xattn_bp")), gate=cols(g("L3_ffn_gate_w").T),
        wg=cols(both(g("L3_ffn_expert_gate").reshape(-1, D), g("L3_ffn_shared_gate")).T),
        wu=cols(both(g("L3_ffn_expert_up").reshape(-1, D), g("L3_ffn_shared_up")).T), wd=cols(down))

    ctx = g("ctx_2048")
    mask = np.zeros((B, P, P, 4), np.uint8)
    mask[..., 0] = g("mask_BxS2_bk0").view(np.uint8)[:, None, :]
    arrays = {
        "x": np.ascontiguousarray(g("x")), "ctx": np.ascontiguousarray(ctx),
        "ctx_T": np.ascontiguousarray(ctx.transpose(0, 2, 1).reshape(B, DC, P, P).transpose(0, 2, 1, 3)),
        "mask": mask.view(np.int32)[..., 0],
    }
    for n in _NAMES:
        arrays[n] = pack(layouts[n], packs[n])
    nc = bacc.Bacc("TRN2", target_bir_lowering=False, num_devices=1)
    t = {n: nc.dram_tensor("in_" + n, v.shape, mybir.dt.from_np(v.dtype), kind="ExternalInput").ap() for n, v in arrays.items()}
    out = nc.dram_tensor("out_x", [B, P, D], F32, kind="ExternalOutput").ap()
    build(nc, t, t["ctx_T"], out, t)
    r = run(nc, [{"in_" + n: v for n, v in arrays.items()}], core_ids=[0])
    return r.results[0]["out_x"]
```
